# Optimizing a Trainium2 kernel written in Bass

```python
import numpy as np
import jax
import jax.numpy as jnp

def _softmax(x, axis=-1):
    return jax.nn.softmax(x, axis=axis)

def _gelu(x):
    return jax.nn.gelu(x, approximate=True)

def _silu(x):
    return jax.nn.silu(x)

def _sigmoid(x):
    return jax.nn.sigmoid(x)

def _layernorm(x, axis=-1, eps=1e-05):
    m = jnp.mean(x, axis=axis, keepdims=True)
    v = jnp.var(x, axis=axis, keepdims=True)
    return (x - m) / jnp.sqrt(v + eps)

def _scatter_add(tgt, idx, src, axis=0):
    return tgt.at[idx].add(src)

def _segment_sum(src, seg, n):
    return jax.ops.segment_sum(src, seg, n)
kernel_name = 'mk_seq_preln_d1_jaxref_r8_b6d8a0'

def setup_inputs(seed: int=0):
    np.random.seed(seed)
    _w = jnp.asarray

    def _L0_attn_setup():
        import math
        import jax, jax.numpy as jnp
        import numpy as np
        N_HEADS = 16
        ROPE_BASE = 10000.0

        def rotate_half(x):
            x_even = x[..., ::2]
            x_odd = x[..., 1::2]
            return jnp.stack((-x_odd, x_even), axis=-1).reshape(x.shape)

        def rope_cache(seq_len, head_dim, dtype):
            pos = jnp.arange(seq_len, dtype=jnp.float32)
            freqs = 1.0 / ROPE_BASE ** (jnp.arange(0, head_dim, 2, dtype=jnp.float32) / head_dim)
            angles = pos[:, None] * freqs[None, :]
            cos = jnp.repeat(jnp.cos(angles), 2, axis=-1).astype(dtype)
            sin = jnp.repeat(jnp.sin(angles), 2, axis=-1).astype(dtype)
            return (cos, sin)
        key = jax.random.key(seed)
        ks = jax.random.split(key, 5)
        B, S, D = (2, 256, 128)
        scale = 1.0 / math.sqrt(D)
        return {'x': jax.random.normal(ks[0], (B, S, D), dtype=jnp.float32), 'wq': jax.random.normal(ks[1], (D, D), dtype=jnp.float32) * scale, 'wk': jax.random.normal(ks[2], (D, D), dtype=jnp.float32) * scale, 'wv': jax.random.normal(ks[3], (D, D), dtype=jnp.float32) * scale, 'wo': jax.random.normal(ks[4], (D, D), dtype=jnp.float32) * scale}
    _L0_attn_in = _L0_attn_setup()

    def _L0_ffn_setup():
        import jax, jax.numpy as jnp
        import numpy as np
        DIM = 128
        DEPTH = 2
        HEADS = 8
        DIM_HEAD = 64
        WINDOW = 64
        INNER = HEADS * DIM_HEAD
        HID = int(DIM * 4 * 2 / 3)
        B, N = (2, 1024)
        QK_SCALE = 8.0

        def shift_token(t):
            t1, t2 = jnp.split(t, 2, axis=-1)
            t2 = jnp.pad(t2, ((0, 0), (1, 0), (0, 0)))[:, :-1]
            return jnp.concatenate([t1, t2], axis=-1)

        def l2norm(t):
            return t / jnp.clip(jnp.linalg.norm(t, axis=-1, keepdims=True), 1e-12)

        def rotate_half(x):
            x1, x2 = jnp.split(x, 2, axis=-1)
            return jnp.concatenate([-x2, x1], axis=-1)

        def rotary_xpos(q, k):
            n = q.shape[-2]
            half_idx = jnp.arange(0, DIM_HEAD, 2, dtype=jnp.float32)
            inv_freq = 1.0 / 10000.0 ** (half_idx / DIM_HEAD)
            t = jnp.arange(n, dtype=jnp.float32)
            freqs = t[:, None] * inv_freq[None, :]
            freqs = jnp.concatenate([freqs, freqs], axis=-1)
            base = (half_idx + 0.4 * DIM_HEAD) / (1.4 * DIM_HEAD)
            power = (t - n // 2) / float(WINDOW // 2)
            scale = base[None, :] ** power[:, None]
            scale = jnp.concatenate([scale, scale], axis=-1)
            cos, sin = (jnp.cos(freqs), jnp.sin(freqs))
            q = q * cos * scale + rotate_half(q) * sin * scale
            k = k * cos / scale + rotate_half(k) * sin / scale
            return (q, k)

        def local_attention(q, k, v):
            b, h, n, d = q.shape
            w = n // WINDOW
            bq = q.reshape(b, h, w, WINDOW, d) * QK_SCALE
            bk = k.reshape(b, h, w, WINDOW, d)
            bv = v.reshape(b, h, w, WINDOW, d)

            def look_around(t):
                p = jnp.pad(t, ((0, 0), (0, 0), (1, 0), (0, 0), (0, 0)))
                return jnp.concatenate([p[:, :, :w], p[:, :, 1:]], axis=3)
            bk, bv = (look_around(bk), look_around(bv))
            bt = jnp.arange(n).reshape(w, WINDOW)
            btp = jnp.pad(bt, ((1, 0), (0, 0)), constant_values=-1)
            btk = jnp.concatenate([btp[:w], btp[1:]], axis=1)
            sim = jnp.einsum('bhwid,bhwjd->bhwij', bq, bk)
            i = bt[:, :, None]
            j = btk[:, None, :]
            mask = (i < j) | (i > j + WINDOW) | (j == -1)
            sim = jnp.where(mask, -jnp.finfo(sim.dtype).max, sim)
            attn = jax.nn.softmax(sim, axis=-1)
            out = jnp.einsum('bhwij,bhwjd->bhwid', attn, bv)
            return out.reshape(b, h, n, d)

        def _layer(x, wqkv, qs, ksc, wo, lg, lb, w1, b1, w2, b2):
            b, n, _ = x.shape
            h = shift_token(x)
            qkv = h @ wqkv
            q, k, v = jnp.split(qkv, 3, axis=-1)
            to_heads = lambda t: t.reshape(b, n, HEADS, DIM_HEAD).transpose(0, 2, 1, 3)
            q, k, v = (to_heads(q), to_heads(k), to_heads(v))
            q = l2norm(q) * qs
            k = l2norm(k) * ksc
            q, k = rotary_xpos(q, k)
            o = local_attention(q, k, v)
            o = o.transpose(0, 2, 1, 3).reshape(b, n, INNER)
            x = x + o @ wo
            h = shift_token(x)
            mu = h.mean(-1, keepdims=True)
            var = h.var(-1, keepdims=True)
            h = (h - mu) / jnp.sqrt(var + 1e-05) * lg + lb
            h = h @ w1 + b1
            a, g = jnp.split(h, 2, axis=-1)
            h = a * jax.nn.gelu(g, approximate=False)
            x = x + h @ w2 + b2
            return x
        key = jax.random.key(seed)
        ks = jax.random.split(key, 6)
        return {'x': jax.random.normal(ks[0], (B, N, DIM), jnp.float32), 'wqkv': jax.random.normal(ks[1], (DEPTH, DIM, 3 * INNER), jnp.float32) * 0.02, 'q_scale': jnp.ones((DEPTH, DIM_HEAD), jnp.float32), 'k_scale': jnp.ones((DEPTH, DIM_HEAD), jnp.float32), 'wo': jax.random.normal(ks[2], (DEPTH, INNER, DIM), jnp.float32) * 0.02, 'ln_g': jnp.ones((DEPTH, DIM), jnp.float32), 'ln_b': jnp.zeros((DEPTH, DIM), jnp.float32), 'w1': jax.random.normal(ks[3], (DEPTH, DIM, 2 * HID), jnp.float32) * 0.02, 'b1': jnp.zeros((DEPTH, 2 * HID), jnp.float32), 'w2': jax.random.normal(ks[4], (DEPTH, HID, DIM), jnp.float32) * 0.02, 'b2': jnp.zeros((DEPTH, DIM), jnp.float32)}
    _L0_ffn_in = _L0_ffn_setup()
    _d = {'L0_attn_x': _L0_attn_in['x'], 'L0_attn_wq': _L0_attn_in['wq'], 'L0_attn_wk': _L0_attn_in['wk'], 'L0_attn_wv': _L0_attn_in['wv'], 'L0_attn_wo': _L0_attn_in['wo'], 'L0_ffn_wqkv': _L0_ffn_in['wqkv'], 'L0_ffn_q_scale': _L0_ffn_in['q_scale'], 'L0_ffn_k_scale': _L0_ffn_in['k_scale'], 'L0_ffn_wo': _L0_ffn_in['wo'], 'L0_ffn_ln_g': _L0_ffn_in['ln_g'], 'L0_ffn_ln_b': _L0_ffn_in['ln_b'], 'L0_ffn_w1': _L0_ffn_in['w1'], 'L0_ffn_b1': _L0_ffn_in['b1'], 'L0_ffn_w2': _L0_ffn_in['w2'], 'L0_ffn_b2': _L0_ffn_in['b2']}
    _x0 = _d['L0_attn_x']
    _d['L0_attn_x'] = jax.random.normal(jax.random.fold_in(jax.random.key(seed), 1), (16, 512, 128), dtype=_x0.dtype)
    del _x0
    return _d

def reference(L0_attn_x, L0_attn_wq, L0_attn_wk, L0_attn_wv, L0_attn_wo, L0_ffn_wqkv, L0_ffn_q_scale, L0_ffn_k_scale, L0_ffn_wo, L0_ffn_ln_g, L0_ffn_ln_b, L0_ffn_w1, L0_ffn_b1, L0_ffn_w2, L0_ffn_b2):

    def _L0_attn_ref(x, wq, wk, wv, wo):
        import math
        import jax, jax.numpy as jnp
        import numpy as np
        N_HEADS = 16
        ROPE_BASE = 10000.0

        def rotate_half(x):
            x_even = x[..., ::2]
            x_odd = x[..., 1::2]
            return jnp.stack((-x_odd, x_even), axis=-1).reshape(x.shape)

        def rope_cache(seq_len, head_dim, dtype):
            pos = jnp.arange(seq_len, dtype=jnp.float32)
            freqs = 1.0 / ROPE_BASE ** (jnp.arange(0, head_dim, 2, dtype=jnp.float32) / head_dim)
            angles = pos[:, None] * freqs[None, :]
            cos = jnp.repeat(jnp.cos(angles), 2, axis=-1).astype(dtype)
            sin = jnp.repeat(jnp.sin(angles), 2, axis=-1).astype(dtype)
            return (cos, sin)
        B, S, D = x.shape
        H = N_HEADS
        hd = D // H

        def split_heads(t):
            return t.reshape(B, S, H, hd).transpose(0, 2, 1, 3)
        q = split_heads(x @ wq.T)
        k = split_heads(x @ wk.T)
        v = split_heads(x @ wv.T)
        cos, sin = rope_cache(S, hd, x.dtype)
        cos = cos[None, None]
        sin = sin[None, None]
        q = q * cos + rotate_half(q) * sin
        k = k * cos + rotate_half(k) * sin
        scores = jnp.einsum('bhqd,bhkd->bhqk', q, k) / math.sqrt(hd)
        causal_mask = jnp.triu(jnp.ones((S, S), dtype=bool), k=1)
        scores = jnp.where(causal_mask, jnp.finfo(scores.dtype).min, scores)
        pattern = jax.nn.softmax(scores, axis=-1)
        head_out = jnp.einsum('bhqk,bhkd->bhqd', pattern, v)
        merged = head_out.transpose(0, 2, 1, 3).reshape(B, S, D)
        out = merged @ wo.T
        return out

    def _L0_ffn_ref(x, wqkv, q_scale, k_scale, wo, ln_g, ln_b, w1, b1, w2, b2):
        import jax, jax.numpy as jnp
        import numpy as np
        DIM = 128
        DEPTH = 2
        HEADS = 8
        DIM_HEAD = 64
        WINDOW = 64
        INNER = HEADS * DIM_HEAD
        HID = int(DIM * 4 * 2 / 3)
        B, N = (2, 1024)
        QK_SCALE = 8.0

        def shift_token(t):
            t1, t2 = jnp.split(t, 2, axis=-1)
            t2 = jnp.pad(t2, ((0, 0), (1, 0), (0, 0)))[:, :-1]
            return jnp.concatenate([t1, t2], axis=-1)

        def l2norm(t):
            return t / jnp.clip(jnp.linalg.norm(t, axis=-1, keepdims=True), 1e-12)

        def rotate_half(x):
            x1, x2 = jnp.split(x, 2, axis=-1)
            return jnp.concatenate([-x2, x1], axis=-1)

        def rotary_xpos(q, k):
            n = q.shape[-2]
            half_idx = jnp.arange(0, DIM_HEAD, 2, dtype=jnp.float32)
            inv_freq = 1.0 / 10000.0 ** (half_idx / DIM_HEAD)
            t = jnp.arange(n, dtype=jnp.float32)
            freqs = t[:, None] * inv_freq[None, :]
            freqs = jnp.concatenate([freqs, freqs], axis=-1)
            base = (half_idx + 0.4 * DIM_HEAD) / (1.4 * DIM_HEAD)
            power = (t - n // 2) / float(WINDOW // 2)
            scale = base[None, :] ** power[:, None]
            scale = jnp.concatenate([scale, scale], axis=-1)
            cos, sin = (jnp.cos(freqs), jnp.sin(freqs))
            q = q * cos * scale + rotate_half(q) * sin * scale
            k = k * cos / scale + rotate_half(k) * sin / scale
            return (q, k)

        def local_attention(q, k, v):
            b, h, n, d = q.shape
            w = n // WINDOW
            bq = q.reshape(b, h, w, WINDOW, d) * QK_SCALE
            bk = k.reshape(b, h, w, WINDOW, d)
            bv = v.reshape(b, h, w, WINDOW, d)

            def look_around(t):
                p = jnp.pad(t, ((0, 0), (0, 0), (1, 0), (0, 0), (0, 0)))
                return jnp.concatenate([p[:, :, :w], p[:, :, 1:]], axis=3)
            bk, bv = (look_around(bk), look_around(bv))
            bt = jnp.arange(n).reshape(w, WINDOW)
            btp = jnp.pad(bt, ((1, 0), (0, 0)), constant_values=-1)
            btk = jnp.concatenate([btp[:w], btp[1:]], axis=1)
            sim = jnp.einsum('bhwid,bhwjd->bhwij', bq, bk)
            i = bt[:, :, None]
            j = btk[:, None, :]
            mask = (i < j) | (i > j + WINDOW) | (j == -1)
            sim = jnp.where(mask, -jnp.finfo(sim.dtype).max, sim)
            attn = jax.nn.softmax(sim, axis=-1)
            out = jnp.einsum('bhwij,bhwjd->bhwid', attn, bv)
            return out.reshape(b, h, n, d)

        def _layer(x, wqkv, qs, ksc, wo, lg, lb, w1, b1, w2, b2):
            b, n, _ = x.shape
            h = shift_token(x)
            qkv = h @ wqkv
            q, k, v = jnp.split(qkv, 3, axis=-1)
            to_heads = lambda t: t.reshape(b, n, HEADS, DIM_HEAD).transpose(0, 2, 1, 3)
            q, k, v = (to_heads(q), to_heads(k), to_heads(v))
            q = l2norm(q) * qs
            k = l2norm(k) * ksc
            q, k = rotary_xpos(q, k)
            o = local_attention(q, k, v)
            o = o.transpose(0, 2, 1, 3).reshape(b, n, INNER)
            x = x + o @ wo
            h = shift_token(x)
            mu = h.mean(-1, keepdims=True)
            var = h.var(-1, keepdims=True)
            h = (h - mu) / jnp.sqrt(var + 1e-05) * lg + lb
            h = h @ w1 + b1
            a, g = jnp.split(h, 2, axis=-1)
            h = a * jax.nn.gelu(g, approximate=False)
            x = x + h @ w2 + b2
            return x
        for l in range(DEPTH):
            x = _layer(x, wqkv[l], q_scale[l], k_scale[l], wo[l], ln_g[l], ln_b[l], w1[l], b1[l], w2[l], b2[l])
        return x
    x = L0_attn_x
    x = x + _L0_attn_ref(_layernorm(x, axis=-1), L0_attn_wq, L0_attn_wk, L0_attn_wv, L0_attn_wo)
    x = x + _L0_ffn_ref(_layernorm(x, axis=-1), L0_ffn_wqkv, L0_ffn_q_scale, L0_ffn_k_scale, L0_ffn_wo, L0_ffn_ln_g, L0_ffn_ln_b, L0_ffn_w1, L0_ffn_b1, L0_ffn_w2, L0_ffn_b2)
    return x

_drawn_inputs = setup_inputs


def setup_inputs(seed=0):
    import zlib

    import numpy as np

    out = dict(_drawn_inputs(seed))
    spreads = {'L0_ffn_q_scale': (1.0, 0.6),
     'L0_ffn_k_scale': (1.0, 0.6),
     'L0_ffn_ln_g': (1.0, 0.6),
     'L0_ffn_ln_b': (0.0, 0.8),
     'L0_ffn_b1': (0.0, 0.8),
     'L0_ffn_b2': (0.0, 0.468)}
    factors = {'L0_ffn_wqkv': 3.363, 'L0_ffn_wo': 3.37, 'L0_ffn_w1': 6.216, 'L0_ffn_w2': 6.121}
    for name, (base, spread) in spreads.items():
        noise = np.random.default_rng([zlib.crc32(name.encode()), seed]).standard_normal(out[name].shape)
        drawn = base * np.exp(spread * noise) if base else spread * noise
        out[name] = jnp.asarray(drawn.astype(out[name].dtype))
    for name, factor in factors.items():
        out[name] = (out[name] * factor).astype(out[name].dtype)
    return out
```

```python
from contextlib import ExitStack

import numpy as np

import concourse.bass as bass
from concourse import mybir

ALU = mybir.AluOpType
ACT = mybir.ActivationFunctionType
AX = mybir.AxisListType
F32 = mybir.dt.float32
BF16 = mybir.dt.bfloat16

P = 128
B, S, D = 16, 512, 128
NT = S // P
LANES = 2
PAIRS = B // LANES
EPS = 1e-5
H1, E1 = 16, 8
VW = E1 + 1
SPLIT = 3
QK_ROWS = SPLIT * SPLIT * E1
ROWS = QK_ROWS + SPLIT
SEG = {0: (0, 512), 1: (512, 384), 2: (1024, 256), 3: (896, 128)}
SCORES = 1280
SCALE1 = float(1.0 / np.sqrt(E1))
L = 2
H2, E2, WIN = 8, 64, 64
INNER = H2 * E2
PAIR2 = H2 // 2
KEYS = WIN + P
HID = int(D * 4 * 2 / 3)
CH = [(0, 128), (128, 128), (256, HID - 256)]
NEG = -3.0e38
DVE_ORDER = 110


class Signal:

    def __init__(self, nc, ctx, name, n=1, uses=1):
        self.sem = [ctx.enter_context(nc.semaphore(f"{name}_{z}")) for z in range(LANES)]
        self.n, self.uses = n, uses

    def at(self, i, k=1, use=0):
        return i * (self.uses * self.n) + use * self.n + k


class Landed:

    def __init__(self, nc, ctx, name, n=1):
        self.sem = ctx.enter_context(nc.semaphore(name))
        self.n = n

    def before(self, i):
        return i * (16 * self.n)

    def now(self, i):
        return i * (16 * self.n) + 16 * self.n


class Chain:

    def __init__(self, nc, ctx, name, per_pair):
        self.sem = ctx.enter_context(nc.semaphore(name))
        self.per_pair, self.count = per_pair, 0

    def mark(self, ins):
        ins.then_inc(self.sem, 1)
        self.count += 1
        return self.count

    def wait(self, eng, i, mark):
        eng.wait_ge(self.sem, i * self.per_pair + mark)

    def link(self, eng, i, ins):
        self.wait(eng, i, self.mark(ins))


def build(nc, t, out):
    with ExitStack() as ctx:
        def sb(name, shape, dt=F32):
            return ctx.enter_context(nc.sbuf_tensor(name, shape, dt))

        def signal(name, n=1, uses=1):
            return Signal(nc, ctx, name, n, uses)

        def landed(name, n=1):
            return [Landed(nc, ctx, f"{name}{z}", n) for z in range(LANES)]

        ident = sb("ident", [P, P])
        identb = sb("identb", [P, P], BF16)
        causal = sb("causal", [P, P], BF16)
        causal_t = sb("causal_t", [P, P], BF16)
        band = sb("band", [P, KEYS], BF16)
        band0 = sb("band0", [P, KEYS], BF16)
        shift = sb("shift", [P, P])
        corner = sb("corner", [P, P])
        cos1 = sb("cos1", [P, S])
        sin1 = sb("sin1", [P, S])
        w1st = sb("w1st", [P, 6, P])
        rot = sb("rot", [P, L, 4, NT, E2])
        scl = sb("scl", [P, L, 4, E2])
        wqkv = sb("wqkv", [P, L, 3 * INNER])
        wo2 = sb("wo2", [P, L, PAIR2, D])
        w1 = sb("w1", [P, L, 2 * HID])
        w2 = sb("w2", [P, L, 3, D])
        b1 = sb("b1", [P, L, 2, 3])
        b2 = sb("b2", [P, L, D])
        lgb = sb("lgb", [P, L, 2])
        nhalf = sb("nhalf", [P, 2 * H2])
        X = [sb(f"X{z}", [P, NT, D]) for z in range(LANES)]
        Z = [sb(f"Z{z}", [P, NT, D]) for z in range(LANES)]
        XN = [sb(f"XN{z}", [P, NT, D]) for z in range(LANES)]
        XT = [sb(f"XT{z}", [P, S]) for z in range(LANES)]
        ZT = [sb(f"ZT{z}", [P, S]) for z in range(LANES)]
        stats = [sb(f"stats{z}", [P, NT, 12]) for z in range(LANES)]
        mv = [sb(f"mv{z}", [P, NT, 2]) for z in range(LANES)]
        veps = [sb(f"veps{z}", [P, NT]) for z in range(LANES)]
        rstd = [sb(f"rstd{z}", [P, NT]) for z in range(LANES)]
        nmax = [sb(f"nmax{z}", [P, NT, H1]) for z in range(LANES)]
        nres = [sb(f"nres{z}", [P, NT, H1]) for z in range(LANES)]
        nparts = [sb(f"nparts{z}", [P, NT, P], BF16) for z in range(LANES)]
        rec1 = [sb(f"rec1{z}", [P, NT, 4]) for z in range(LANES)]
        V1 = [sb(f"V1{z}", [P, NT, H1 * VW + 32 - VW]) for z in range(LANES)]
        mix = [sb(f"mix{z}", [P, 1536]) for z in range(LANES)]
        qkp = [m[:, :].bitcast(BF16).rearrange("p (w a s) -> p w a s", w=2, a=SPLIT) for m in mix]
        U = [m[:, 0:512] for m in mix]
        MG = [m[:, 512:1024].rearrange("p (t c) -> p t c", t=NT) for m in mix]
        NMT = [m[:, 1024:1280].bitcast(BF16) for m in mix]
        QT = [sb(f"QT{z}", [P, 2, PAIR2, P]) for z in range(LANES)]
        VPB = [sb(f"VPB{z}", [P, 2, PAIR2, P]) for z in range(LANES)]
        ss = [sb(f"ss{z}", [P, 2 * H2]) for z in range(LANES)]
        inv = [sb(f"inv{z}", [P, 2 * H2]) for z in range(LANES)]
        nm2 = [sb(f"nm2{z}", [P, 4]) for z in range(LANES)]
        nb2 = [sb(f"nb2{z}", [P, 4]) for z in range(LANES)]
        sum2 = [sb(f"sum2{z}", [P, 4]) for z in range(LANES)]
        rec2 = [sb(f"rec2{z}", [P, 4]) for z in range(LANES)]
        arr = [sb(f"arr{z}", [P, 8192]) for z in range(LANES)]
        QA = [a[:, 0:4096].bitcast(BF16).rearrange("p (h s) -> p h s", h=H1) for a in arr]
        KA = [a[:, 4096:8192].bitcast(BF16).rearrange("p (h s) -> p h s", h=H1) for a in arr]
        SQ = [a[:, 0:1024].rearrange("p (w c) -> p w c", w=2) for a in arr]
        RC = [a[:, 1024:2048].rearrange("p (w c) -> p w c", w=2) for a in arr]
        RS = [a[:, 2048:3072].rearrange("p (w c) -> p w c", w=2) for a in arr]
        QR = [a[:, 3072:4096].rearrange("p (w c) -> p w c", w=2) for a in arr]
        PR = [a[:, 4096:4864].rearrange("p (h c) -> p h c", h=4) for a in arr]
        PM = [a[:, 6144:6656].rearrange("p (h c) -> p h c", h=4) for a in arr]
        PP = [a[:, 6656:6912].rearrange("p (h c) -> p h c", h=4) for a in arr]
        PTM = [a[:, 4864:5376] for a in arr]
        PTP = [a[:, 5376:5632] for a in arr]
        OT = [a[:, 5632:6144].rearrange("p (j q) -> p j q", j=PAIR2) for a in arr]
        prob = [sb(f"prob{z}", [P, 4 * SCORES]) for z in range(LANES)]
        PT1 = [p[:, :].rearrange("p (b c) -> p b c", b=4) for p in prob]
        KT = [p[:, 0:PAIR2 * (WIN + S)].rearrange("p (j s) -> p j s", j=PAIR2) for p in prob]
        V2 = [p[:, 2304:2816] for p in prob]
        G = [p[:, 2816:2816 + 3 * S].rearrange("p (c s) -> p c s", c=3) for p in prob]
        rope_s = [p[:, 0:1024].rearrange("p (w c) -> p w c", w=2) for p in prob]
        rope_t = [p[:, 1024:2048].rearrange("p (w c) -> p w c", w=2) for p in prob]

        ps = ctx.enter_context(nc.psum_tensor("ps", [P, 8, 512], F32))
        bank = [[ps[:, 4 * z + n, :] for n in range(4)] for z in range(LANES)]
        region = [ps[:, 4 * z:4 * z + 3, :].rearrange("p b c -> p (b c)") for z in range(LANES)]
        parts_dram = [nc.dram_tensor(f"parts{z}", (2, SPLIT * E1, H1 * S), BF16, kind="Internal").ap()
                      for z in range(LANES)]

        consts = ctx.enter_context(nc.semaphore("consts"))
        made = ctx.enter_context(nc.semaphore("made"))
        tables = ctx.enter_context(nc.semaphore("tables"))
        x_in = landed("x_in")
        ln_var = signal("ln_var", uses=2 + L)
        ln_rstd = signal("ln_rstd", uses=2 + L)
        ln_out = signal("ln_out", uses=2 + L)
        tr_done = signal("tr_done", uses=2 + L)
        xt_ready = signal("xt_ready", uses=2 + L)
        proj = signal("proj", n=4)
        v1_done = signal("v1_done")
        v1_ready = signal("v1_ready")
        roped = signal("roped", n=2)
        rope_sum = signal("rope_sum", n=2)
        part_hi = signal("part_hi", n=2)
        part_res = signal("part_res", n=2)
        part_mid = signal("part_mid", n=2)
        parts = signal("parts", n=2)
        stored = [landed("stored_q"), landed("stored_k")]
        laid = landed("laid", 2 * SPLIT + 1)
        scored = signal("scored", n=H1)
        maxed = signal("maxed", n=H1)
        nm_parts = signal("nm_parts")
        nm_tr = signal("nm_tr")
        nmt_ready = signal("nmt_ready")
        nm_laid = landed("nm_laid", SPLIT)
        scored_t = signal("scored_t", n=H1)
        exped = signal("exped", n=H1)
        pv_done = signal("pv_done", n=H1 // 2)
        u_ready = signal("u_ready", n=4)
        u_tr = signal("u_tr", n=4)
        mg_ready = signal("mg_ready", n=4)
        wo_done = signal("wo_done")
        x1_ready = signal("x1_ready")
        zt_tr = signal("zt_tr", uses=L)
        zt_ready = signal("zt_ready", uses=L)
        qk_done = signal("qk_done", n=NT, uses=L)
        v_done = signal("v_done", n=NT, uses=L)
        k_squared = signal("k_squared", n=NT, uses=L)
        squared = signal("squared", n=NT, uses=L)
        q_rot = signal("q_rot", n=NT, uses=L)
        rot_done = signal("rot_done", n=NT, uses=L)
        ss_ready = signal("ss_ready", n=NT, uses=L)
        inv_ready = signal("inv_ready", n=NT, uses=L)
        q_ready = signal("q_ready", n=NT, uses=L)
        k_ready = signal("k_ready", n=NT, uses=L)
        q_tr = signal("q_tr", n=NT, uses=L)
        k_tr = signal("k_tr", n=NT, uses=L)
        qt_ready = signal("qt_ready", n=NT, uses=L)
        kt_ready = signal("kt_ready", n=NT, uses=L)
        pad_ready = signal("pad_ready", uses=L)
        v2_ready = signal("v2_ready", n=NT, uses=L)
        s2_done = signal("s2_done", n=2 * NT, uses=L)
        nb2_ready = signal("nb2_ready", n=2 * NT, uses=L)
        exp2 = signal("exp2", n=2 * NT, uses=L)
        p_ready = signal("p_ready", n=2 * NT, uses=L)
        p_tr = signal("p_tr", n=2 * NT, uses=L)
        ptm_ready = signal("ptm_ready", n=2 * NT, uses=L)
        ptp_ready = signal("ptp_ready", n=2 * (NT - 1), uses=L)
        pv2 = signal("pv2", n=2 * NT, uses=L)
        ot_ready = signal("ot_ready", n=2 * NT, uses=L)
        wo2_done = signal("wo2_done", n=NT, uses=L)
        z_acc = signal("z_acc", n=NT, uses=L)
        shifted = signal("shifted", uses=L)
        z_b2 = signal("z_b2", uses=L)
        gate_mm = signal("gate_mm", n=3, uses=L)
        gelu = signal("gelu", n=3, uses=L)
        up_mm = signal("up_mm", n=3, uses=L)
        hid = signal("hid", n=3, uses=L)
        down_mm = signal("down_mm", uses=L)
        z_out = signal("z_out", uses=L)
        fin = signal("fin")
        y_out = landed("y_out")
        N_CONST = 17
        N_MADE = 5 * LANES + 1

        block = ctx.enter_context(nc.Block())

        @block.sync
        def _(sp):
            for dst, src in (
                (w1st[:, :, :], t["w1st"]), (ident[:, :], t["ident"]), (identb[:, :], t["identb"]),
                (cos1[:, :], t["cos1"]), (sin1[:, :], t["sin1"]), (causal[:, :], t["causal"]),
                (causal_t[:, :], t["causal_t"]), (band[:, :], t["band"]), (band0[:, :], t["band0"]),
                (shift[:, :], t["shift"]), (corner[:, :], t["corner"]),
                (wqkv[:, :, :], t["wqkv"].rearrange("l d n -> d l n")),
                (wo2[:, :, :, :], t["wo2"].rearrange("l (j p) n -> p l j n", p=P)),
                (w1[:, :, :], t["w1"].rearrange("l d n -> d l n")),
                (b2[:, :, :], t["b2"].rearrange("(o l) n -> o l n", o=1).to_broadcast([P, L, D])),
                (lgb[:, :, :], t["lgb"]),
                (b1[:, :, :, :], t["b1"]),
            ):
                sp.dma_start(dst, src).then_inc(consts, 16)
            for l in range(L):
                for c, (c0, w) in enumerate(CH):
                    sp.dma_start(w2[0:w, l, c, :], t["w2"][l, c0:c0 + w, :]).then_inc(consts, 16)
                sp.dma_start(rot[:, l, :, :, :], t["rot"]).then_inc(consts, 16)
                for n in range(4):
                    sp.dma_start(scl[:, l, n, :],
                                 t["scl"][l:l + 1, n, :].to_broadcast([P, E2])).then_inc(consts, 16)
            with sp.Fori(0, PAIRS) as i:
                row = [sp.snap(i * LANES + z) for z in range(LANES)]
                for z in range(LANES):
                    batch = row[z]
                    sp.dma_start(X[z][:, :, :],
                                 t["x"][batch].rearrange("(t p) d -> p t d", p=P)).then_inc(x_in[z].sem, 16)
                for z in range(LANES):
                    for w in range(2):
                        sp.wait_ge(parts.sem[z], parts.at(i, w + 1))
                        sp.dma_start(parts_dram[z][w].rearrange("(a p) (h s) -> (p h) a s", a=SPLIT, h=H1),
                                     qkp[z][:, w, :, :]).then_inc(stored[w][z].sem, 16)
                for z in range(LANES):
                    for w in range(2):
                        sp.wait_ge(stored[w][z].sem, stored[w][z].now(i))
                        for a in range(SPLIT):
                            r0 = a * SPLIT * E1
                            if w == 0:
                                src = parts_dram[z][0, a * E1:(a + 1) * E1, :]
                                src = src.rearrange("(o p) c -> o p c", o=1).to_broadcast([SPLIT, E1, H1 * S])
                                dst = QA[z][r0:r0 + SPLIT * E1, :, :]
                            else:
                                src = parts_dram[z][1]
                                dst = KA[z][r0:r0 + SPLIT * E1, :, :]
                            sp.dma_start(dst, src).then_inc(laid[z].sem, 16)
                    sp.dma_start(KA[z][QK_ROWS:ROWS, :, :], t["ones"]).then_inc(laid[z].sem, 16)
                for z in range(LANES):
                    sp.wait_ge(nmt_ready.sem[z], nmt_ready.at(i, 1))
                    for a in range(SPLIT):
                        sp.dma_start(QA[z][QK_ROWS + a:QK_ROWS + a + 1, :, :],
                                     NMT[z][a * H1:(a + 1) * H1, :]).then_inc(nm_laid[z].sem, 16)
                for z in range(LANES):
                    batch = row[z]
                    sp.wait_ge(fin.sem[z], fin.at(i, 1))
                    sp.dma_start(out[batch].rearrange("(t p) d -> p t d", p=P),
                                 XN[z][:, :, :]).then_inc(y_out[z].sem, 16)
            for z in range(LANES):
                sp.wait_ge(y_out[z].sem, 1 + 16 * PAIRS)

        @block.tensor
        def _(pe):
            pe.wait_ge(consts, 16 * (N_CONST + L * 8))
            pe.wait_ge(made, N_MADE)

            def turn(dst, src, n=NT):
                for tt in range(n):
                    last = pe.transpose(dst[:, tt * P:(tt + 1) * P], src(tt), ident[:, :])
                return last

            with pe.Fori(0, PAIRS) as i:
                for z in range(LANES):
                    pe.wait_ge(ln_out.sem[z], ln_out.at(i, 1, 0))
                    turn(bank[z][3], lambda tt: XN[z][:, tt, :]).then_inc(tr_done.sem[z], 1)
                for z in range(LANES):
                    pe.wait_ge(xt_ready.sem[z], xt_ready.at(i, 1, 0))
                    for n in range(4):
                        pe.matmul(bank[z][n], w1st[:, n, :], XT[z][:, :], start=True,
                                  stop=True).then_inc(proj.sem[z], 1)
                for z in range(LANES):
                    pe.wait_ge(roped.sem[z], roped.at(i, 1))
                    for tt in range(NT):
                        last = pe.matmul(bank[z][0][:, tt * P:(tt + 1) * P], XT[z][:, tt * P:(tt + 1) * P],
                                         w1st[:, 4, :], start=True, stop=True)
                    last.then_inc(v1_done.sem[z], 1)
                for h in range(H1):
                    for z in range(LANES):
                        if h == 0:
                            pe.wait_ge(v1_ready.sem[z], v1_ready.at(i, 1))
                            pe.wait_ge(roped.sem[z], roped.at(i, 2))
                            pe.wait_ge(laid[z].sem, laid[z].now(i))
                        else:
                            pe.wait_ge(maxed.sem[z], maxed.at(i, h))
                        for r in range(NT):
                            qt = NT - 1 - r
                            c0, w = SEG[r]
                            pe.matmul(region[z][:, c0:c0 + w], QA[z][0:QK_ROWS, h, qt * P:(qt + 1) * P],
                                      KA[z][0:QK_ROWS, h, 0:w], start=True, stop=False)
                            last = pe.matmul(region[z][:, c0 + w - P:c0 + w], identb[:, :], causal[:, :],
                                             start=False, stop=True)
                        last.then_inc(scored.sem[z], 1)
                for z in range(LANES):
                    pe.wait_ge(nm_parts.sem[z], nm_parts.at(i, 1))
                    tp = bank[z][3][:, 0:256].bitcast(BF16)
                    for tt in range(NT):
                        last = pe.transpose(tp[:, tt * P:(tt + 1) * P],
                                            nparts[z][:, tt, :], identb[:, :])
                    last.then_inc(nm_tr.sem[z], 1)

                def values(j):
                    for z in range(LANES):
                        if j == 0:
                            pe.wait_ge(nmt_ready.sem[z], nmt_ready.at(i, 1))
                        elif j % 2 == 0:
                            pe.wait_ge(mg_ready.sem[z], mg_ready.at(i, j // 2))
                        pe.wait_ge(exped.sem[z], exped.at(i, 2 * j + 2))
                    for kt in range(NT):
                        c0, w = SEG[kt]
                        for z in range(LANES):
                            for s in range(2):
                                h = 2 * j + s
                                q0 = 32 * ((h + 2 * z) % 4)
                                last = pe.matmul(bank[z][3][q0:q0 + 32, kt * P:S],
                                                 V1[z][:, kt, h * VW:h * VW + 32],
                                                 PT1[z][:, h % 4, c0:c0 + w], start=(kt == 0), stop=(kt == NT - 1))
                            if kt == NT - 1:
                                last.then_inc(pv_done.sem[z], 1)

                def heads_out(g):
                    for z in range(LANES):
                        pe.wait_ge(u_ready.sem[z], u_ready.at(i, g + 1))
                        turn(bank[z][3], lambda tt: U[z][:, tt * P:(tt + 1) * P]).then_inc(u_tr.sem[z], 1)

                for h in range(H1):
                    for z in range(LANES):
                        if h == 0:
                            pe.wait_ge(maxed.sem[z], maxed.at(i, H1))
                            pe.wait_ge(nm_laid[z].sem, nm_laid[z].now(i))
                        else:
                            pe.wait_ge(exped.sem[z], exped.at(i, h))
                        for kt in range(NT):
                            c0, w = SEG[kt]
                            pe.matmul(region[z][:, c0:c0 + w], KA[z][0:ROWS, h, kt * P:(kt + 1) * P],
                                      QA[z][0:ROWS, h, kt * P:S], start=True, stop=False)
                            last = pe.matmul(region[z][:, c0:c0 + P], identb[:, :], causal_t[:, :],
                                             start=False, stop=True)
                        last.then_inc(scored_t.sem[z], 1)
                    if h % 2 == 0 and h >= 2:
                        values(h // 2 - 1)
                    if h % 4 == 1 and h >= 5:
                        heads_out(h // 4 - 1)
                values(H1 // 2 - 1)
                heads_out(3)
                for z in range(LANES):
                    pe.wait_ge(mg_ready.sem[z], mg_ready.at(i, 4))
                    pe.wait_ge(exped.sem[z], exped.at(i, H1))
                    turn(bank[z][0], lambda tt: MG[z][:, tt, :]).then_inc(tr_done.sem[z], 1)
                for z in range(LANES):
                    pe.wait_ge(xt_ready.sem[z], xt_ready.at(i, 1, 1))
                    for tt in range(NT):
                        last = pe.matmul(bank[z][1][:, tt * P:(tt + 1) * P], XT[z][:, tt * P:(tt + 1) * P],
                                         w1st[:, 5, :], start=True, stop=True)
                    last.then_inc(wo_done.sem[z], 1)

                for l in range(L):
                    for z in range(LANES):
                        if l == 0:
                            pe.wait_ge(ln_out.sem[z], ln_out.at(i, 1, 1))
                        else:
                            pe.wait_ge(z_out.sem[z], z_out.at(i, 1, l - 1))
                        turn(bank[z][0], lambda tt: Z[z][:, tt, :]).then_inc(zt_tr.sem[z], 1)
                    for tt in range(NT):
                        tok = slice(tt * P, (tt + 1) * P)
                        for z in range(LANES):
                            if tt == 0:
                                pe.wait_ge(zt_ready.sem[z], zt_ready.at(i, 1, l))
                            else:
                                pe.wait_ge(ot_ready.sem[z], ot_ready.at(i, 2 * tt, l))
                                pe.wait_ge(z_acc.sem[z], z_acc.at(i, tt, l))
                            for n in range(3):
                                mm = pe.matmul(bank[z][n], ZT[z][:, tok], wqkv[:, l, n * INNER:(n + 1) * INNER],
                                               start=True, stop=True)
                                if n == 1:
                                    mm.then_inc(qk_done.sem[z], 1)
                            mm.then_inc(v_done.sem[z], 1)
                        for z in range(LANES):
                            pe.wait_ge(q_ready.sem[z], q_ready.at(i, tt + 1, l))
                            if tt:
                                pe.wait_ge(ptm_ready.sem[z], ptm_ready.at(i, 2 * tt, l))
                            turn(bank[z][3], lambda j: QR[z][:, 0, j * P:(j + 1) * P]).then_inc(q_tr.sem[z], 1)
                            pe.wait_ge(k_ready.sem[z], k_ready.at(i, tt + 1, l))
                            pe.wait_ge(squared.sem[z], squared.at(i, tt + 1, l))
                            pe.wait_ge(rot_done.sem[z], rot_done.at(i, tt + 1, l))
                            turn(bank[z][0], lambda j: QR[z][:, 1, j * P:(j + 1) * P]).then_inc(k_tr.sem[z], 1)
                        for half in range(2):
                            u = 2 * tt + half + 1
                            for z in range(LANES):
                                if half == 0:
                                    pe.wait_ge(qt_ready.sem[z], qt_ready.at(i, tt + 1, l))
                                    pe.wait_ge(kt_ready.sem[z], kt_ready.at(i, tt + 1, l))
                                    pe.wait_ge(v2_ready.sem[z], v2_ready.at(i, tt + 1, l))
                                    if tt == 0:
                                        pe.wait_ge(pad_ready.sem[z], pad_ready.at(i, 1, l))
                                else:
                                    pe.wait_ge(exp2.sem[z], exp2.at(i, u - 1, l))
                                for n in range(4):
                                    h = 4 * half + n
                                    dst = bank[z][1 + n // 2][:, (n % 2) * KEYS:(n % 2 + 1) * KEYS]
                                    pe.matmul(dst, QT[z][:, h % 2, h // 2, :], KT[z][:, h // 2, tt * P:tt * P + KEYS],
                                              start=True, stop=False)
                                    mm = pe.matmul(dst, identb[:, :], (band if tt else band0)[:, :],
                                                   start=False, stop=True)
                                mm.then_inc(s2_done.sem[z], 1)
                            for z in range(LANES):
                                pe.wait_ge(p_ready.sem[z], p_ready.at(i, u, l))
                                if half:
                                    pe.wait_ge(ot_ready.sem[z], ot_ready.at(i, u - 1, l))
                                for n in range(4):
                                    mm = pe.transpose(bank[z][3][:, n * P:(n + 1) * P], PM[z][:, n, :], ident[:, :])
                                if tt:
                                    for n in range(2):
                                        mm = pe.transpose(bank[z][0][:, n * P:(n + 1) * P],
                                                          PP[z][:, 2 * n:2 * n + 2, :].rearrange("p h c -> p (h c)"), ident[:, :])
                                mm.then_inc(p_tr.sem[z], 1)
                            for z in range(LANES):
                                pe.wait_ge(ptm_ready.sem[z], ptm_ready.at(i, u, l))
                                if tt:
                                    pe.wait_ge(ptp_ready.sem[z], ptp_ready.at(i, u - 2, l))
                                for n in range(2):
                                    j = 2 * half + n
                                    dst = bank[z][0][:, 256 + n * P:256 + (n + 1) * P]
                                    for s in range(2):
                                        mm = pe.matmul(dst[s * E2:(s + 1) * E2, :],
                                                       V2[z][:, (2 * j + s) * E2:(2 * j + s + 1) * E2],
                                                       PTM[z][:, (2 * n + s) * P:(2 * n + s + 1) * P],
                                                       start=True, stop=(tt == 0))
                                    if tt:
                                        mm = pe.matmul(dst, VPB[z][:, (tt - 1) % 2, j, :], PTP[z][:, n * P:(n + 1) * P],
                                                       start=False, stop=True)
                                mm.then_inc(pv2.sem[z], 1)
                        for z in range(LANES):
                            pe.wait_ge(ot_ready.sem[z], ot_ready.at(i, 2 * tt + 2, l))
                            for j in range(PAIR2):
                                mm = pe.matmul(bank[z][1][:, 0:D], OT[z][:, j, :], wo2[:, l, j, :],
                                               start=(j == 0), stop=(j == PAIR2 - 1))
                            mm.then_inc(wo2_done.sem[z], 1)
                    for z in range(LANES):
                        pe.wait_ge(z_acc.sem[z], z_acc.at(i, NT, l))
                        pe.matmul(bank[z][2][:, 0:NT * 64], shift[:, :], Z[z][:, :, 64:128], start=True, stop=True)
                        pe.matmul(bank[z][2][:, 64:NT * 64], corner[:, :], Z[z][:, 0:NT - 1, 64:128], start=False,
                                  stop=True, skip_group_check=True).then_inc(shifted.sem[z], 1)
                    for z in range(LANES):
                        pe.wait_ge(ln_out.sem[z], ln_out.at(i, 1, 2 + l))
                        turn(bank[z][0], lambda tt: XN[z][:, tt, :]).then_inc(tr_done.sem[z], 1)
                    for z in range(LANES):
                        pe.wait_ge(xt_ready.sem[z], xt_ready.at(i, 1, 2 + l))
                        for c, (c0, w) in enumerate(CH):
                            pe.matmul(bank[z][1 + c][0:w, :], w1[:, l, HID + c0:HID + c0 + w], XT[z][:, :],
                                      start=True, stop=True).then_inc(gate_mm.sem[z], 1)
                    for z in range(LANES):
                        for c, (c0, w) in enumerate(CH):
                            if c:
                                pe.wait_ge(gelu.sem[z], gelu.at(i, c, l))
                            pe.matmul(bank[z][c][0:w, :], w1[:, l, c0:c0 + w], XT[z][:, :],
                                      start=True, stop=True).then_inc(up_mm.sem[z], 1)
                    for z in range(LANES):
                        pe.wait_ge(hid.sem[z], hid.at(i, 3, l))
                        for tt in range(NT):
                            for c, (c0, w) in enumerate(CH):
                                mm = pe.matmul(bank[z][3][:, tt * P:(tt + 1) * P], G[z][0:w, c, tt * P:(tt + 1) * P],
                                               w2[0:w, l, c, :], start=(c == 0), stop=(c == 2))
                        mm.then_inc(down_mm.sem[z], 1)

        @block.vector
        def _(v):
            v.wait_ge(consts, 16 * (N_CONST + L * 8))
            for l in range(L):
                for n in range(4):
                    m = v.tensor_tensor(rot[:, l, n, :, :], rot[:, l, n, :, :],
                                        scl[:, l, n:n + 1, :].to_broadcast([P, NT, E2]), ALU.mult)
            m.then_inc(tables, 1)
            v.wait_ge(tables, 1)
            v.wait_ge(made, N_MADE)
            chain = Chain(nc, ctx, "dve_order", DVE_ORDER)

            with v.Fori(0, PAIRS) as i:
                def moments(pieces):
                    counted = []
                    for z in range(LANES):
                        for tt in range(NT):
                            n = len(pieces(z, tt))
                            for m, piece in enumerate(pieces(z, tt)):
                                if z == 1 and tt == NT - 1 and m == n - 1:
                                    chain.wait(v, i, counted[0])
                                ins = v.bn_stats(stats[z][:, tt, 6 * m:6 * m + 6], piece)
                        counted.append(chain.mark(ins))
                    for z in range(LANES):
                        for tt in range(NT):
                            ins = v.bn_aggr(mv[z][:, tt, :], stats[z][:, tt, 0:6 * n])
                        chain.link(v, i, ins)
                        if z == 0:
                            chain.wait(v, i, counted[1])
                        v.tensor_scalar(veps[z][:, :], mv[z][:, :, 1], EPS, None, ALU.add).then_inc(ln_var.sem[z], 1)

                def normalise(z, dst, pieces, use):
                    v.wait_ge(ln_rstd.sem[z], ln_rstd.at(i, 1, use))
                    for tt in range(NT):
                        c = 0
                        for piece in pieces(z, tt):
                            w = piece.shape[-1]
                            ins = v.tensor_scalar(dst[z][:, tt, c:c + w], piece, mv[z][:, tt, 0:1],
                                                  rstd[z][:, tt:tt + 1], ALU.subtract, ALU.mult)
                            c += w
                    ins.then_inc(ln_out.sem[z], 1)

                for z in range(LANES):
                    v.wait_ge(x_in[z].sem, x_in[z].now(i))
                moments(lambda z, tt: [X[z][:, tt, :]])
                for z in range(LANES):
                    v.wait_ge(y_out[z].sem, 1 + y_out[z].before(i))
                    normalise(z, XN, lambda z, tt: [X[z][:, tt, :]], 0)
                for z in range(LANES):
                    for w in range(2):
                        v.wait_ge(proj.sem[z], proj.at(i, 2 * w + 2))
                        v.tensor_tensor(rope_t[z][:, w, :], bank[z][2 * w], cos1[:, :], ALU.mult)
                        v.tensor_tensor(rope_s[z][:, w, :], bank[z][2 * w + 1], sin1[:, :],
                                        ALU.mult).then_inc(roped.sem[z], 1)
                for z in range(LANES):
                    for w in range(2):
                        v.wait_ge(roped.sem[z], roped.at(i, w + 1))
                        v.tensor_tensor(rope_t[z][:, w, :], rope_t[z][:, w, :], rope_s[z][:, w, :],
                                        ALU.add).then_inc(rope_sum.sem[z], 1)
                for z in range(LANES):
                    for w in range(2):
                        v.wait_ge(part_hi.sem[z], part_hi.at(i, w + 1))
                        v.tensor_tensor(rope_s[z][:, w, :], rope_t[z][:, w, :], qkp[z][:, w, 0, :],
                                        ALU.subtract).then_inc(part_res.sem[z], 1)
                for z in range(LANES):
                    for w in range(2):
                        v.wait_ge(part_mid.sem[z], part_mid.at(i, w + 1))
                        v.tensor_tensor(qkp[z][:, w, 2, :], rope_s[z][:, w, :], qkp[z][:, w, 1, :],
                                        ALU.subtract).then_inc(parts.sem[z], 1)
                for h in range(H1):
                    for z in range(LANES):
                        v.wait_ge(scored.sem[z], scored.at(i, h + 1))
                        for r in range(NT):
                            c0, w = SEG[r]
                            ins = v.tensor_reduce(nmax[z][:, NT - 1 - r, h:h + 1], region[z][:, c0:c0 + w], AX.X,
                                                  ALU.max, negate=True)
                        ins.then_inc(maxed.sem[z], 1)
                for z in range(LANES):
                    v.wait_ge(maxed.sem[z], maxed.at(i, H1))
                    chain.link(v, i, v.tensor_copy(nparts[z][:, :, 0:H1], nmax[z][:, :, :]))
                    chain.link(v, i, v.tensor_tensor(nres[z][:, :, :], nmax[z][:, :, :], nparts[z][:, :, 0:H1],
                                                     ALU.subtract))
                    chain.link(v, i, v.tensor_copy(nparts[z][:, :, 1 * H1:2 * H1], nres[z][:, :, :]))
                    v.tensor_tensor(nparts[z][:, :, 2 * H1:3 * H1], nres[z][:, :, :], nparts[z][:, :, 1 * H1:2 * H1],
                                    ALU.subtract).then_inc(nm_parts.sem[z], 1)
                for g in range(4):
                    for z in range(LANES):
                        v.wait_ge(u_tr.sem[z], u_tr.at(i, g + 1))
                        heads = bank[z][3].rearrange("p (t c e) -> p t c e", t=NT, c=4)
                        chain.link(v, i, v.reciprocal(rec1[z][:, :, :], heads[:, :, :, E1]))
                        for half in range(2):
                            c = (2 * half + 2 * z) % 4
                            dst = MG[z][:, :, (4 * g + 2 * half) * E1:(4 * g + 2 * half + 2) * E1]
                            ins = v.tensor_tensor(dst.rearrange("p t (c e) -> p t c e", c=2),
                                                  heads[:, :, c:c + 2, 0:E1],
                                                  rec1[z][:, :, c:c + 2].unsqueeze(3).to_broadcast([P, NT, 2, E1]),
                                                  ALU.mult)
                        ins.then_inc(mg_ready.sem[z], 1)
                for z in range(LANES):
                    v.wait_ge(wo_done.sem[z], wo_done.at(i, 1))
                    v.tensor_tensor(X[z][:, :, :].rearrange("p t d -> p (t d)"), bank[z][1],
                                    X[z][:, :, :].rearrange("p t d -> p (t d)"), ALU.add).then_inc(x1_ready.sem[z], 1)
                for z in range(LANES):
                    v.wait_ge(x1_ready.sem[z], x1_ready.at(i, 1))
                moments(lambda z, tt: [X[z][:, tt, :]])
                for z in range(LANES):
                    normalise(z, Z, lambda z, tt: [X[z][:, tt, :]], 1)

                for l in range(L):
                    for z in range(LANES):
                        v.memset(KT[z][:, :, 0:WIN], 0.0).then_inc(pad_ready.sem[z], 1)
                    for tt in range(NT):
                        for z in range(LANES):
                            v.wait_ge(qk_done.sem[z], qk_done.at(i, tt + 1, l))
                            if tt:
                                v.wait_ge(k_ready.sem[z], k_ready.at(i, tt, l))
                            for w in range(2):
                                if w:
                                    v.wait_ge(k_squared.sem[z], k_squared.at(i, tt + 1, l))
                                src = bank[z][w].rearrange("p (h e) -> p h e", h=H2)
                                dc = RC[z][:, w, :].rearrange("p (h e) -> p h e", h=H2)
                                ds = RS[z][:, w, :].rearrange("p (h e) -> p h e", h=H2)
                                v.tensor_tensor(dc, src, rot[:, l, 2 * w, tt:tt + 1, :].to_broadcast([P, H2, E2]),
                                                ALU.mult)
                                for s in range(2):
                                    o, n = 32 * s, 32 * (1 - s)
                                    ins = v.tensor_tensor(
                                        ds[:, :, o:o + 32], src[:, :, n:n + 32],
                                        rot[:, l, 2 * w + 1, tt:tt + 1, o:o + 32].to_broadcast([P, H2, 32]), ALU.mult)
                                ins.then_inc((rot_done if w else q_rot).sem[z], 1)
                            v.wait_ge(squared.sem[z], squared.at(i, tt + 1, l))
                            chain.link(v, i, v.tensor_reduce(
                                ss[z][:, :], SQ[z][:, :, :].rearrange("p w (h e) -> p (w h) e", e=E2), AX.X, ALU.add))
                            v.tensor_scalar(ss[z][:, :], ss[z][:, :], 1e-24, None, ALU.max).then_inc(ss_ready.sem[z], 1)
                        for z in range(LANES):
                            v.wait_ge(q_tr.sem[z], q_tr.at(i, tt + 1, l))
                            for s in range(2):
                                ins = v.tensor_copy(QT[z][s * E2:(s + 1) * E2, s, :, :],
                                                    bank[z][3][s * E2:(s + 1) * E2, :].rearrange("p (j q) -> p j q", j=PAIR2))
                            ins.then_inc(qt_ready.sem[z], 1)
                        for half in range(2):
                            u = 2 * tt + half + 1
                            for z in range(LANES):
                                v.wait_ge(s2_done.sem[z], s2_done.at(i, u, l))
                                v.wait_ge(inv_ready.sem[z], inv_ready.at(i, tt + 1, l))
                                if u > 1:
                                    v.wait_ge(exp2.sem[z], exp2.at(i, u - 1, l))
                                for n in range(2):
                                    ins = v.tensor_reduce(nm2[z][:, 2 * n:2 * n + 2],
                                                          bank[z][1 + n][:, 0:2 * KEYS].rearrange("p (h c) -> p h c", h=2),
                                                          AX.X, ALU.max, negate=True)
                                chain.link(v, i, ins)
                                v.tensor_tensor(nb2[z][:, :], nm2[z][:, :], inv[z][:, 4 * half:4 * half + 4],
                                                ALU.mult).then_inc(nb2_ready.sem[z], 1)
                            for z in range(LANES):
                                v.wait_ge(exp2.sem[z], exp2.at(i, u, l))
                                chain.link(v, i, v.reciprocal(rec2[z][:, :], sum2[z][:, :]))
                                if u > 1:
                                    v.wait_ge(p_tr.sem[z], p_tr.at(i, u - 1, l))
                                if tt:
                                    v.tensor_tensor(PP[z][:, :, :], PR[z][:, :, 0:WIN],
                                                    rec2[z][:, :].unsqueeze(2).to_broadcast([P, 4, WIN]), ALU.mult)
                                v.tensor_tensor(PM[z][:, :, :], PR[z][:, :, WIN:KEYS],
                                                rec2[z][:, :].unsqueeze(2).to_broadcast([P, 4, P]),
                                                ALU.mult).then_inc(p_ready.sem[z], 1)
                            for z in range(LANES if tt else 0):
                                v.wait_ge(p_tr.sem[z], p_tr.at(i, u, l))
                                v.tensor_copy(PTP[z][:, :], bank[z][0][:, 0:256]).then_inc(ptp_ready.sem[z], 1)
                        for z in range(LANES):
                            v.wait_ge(wo2_done.sem[z], wo2_done.at(i, tt + 1, l))
                            v.tensor_tensor(Z[z][:, tt, :], bank[z][1][:, 0:D], Z[z][:, tt, :],
                                            ALU.add).then_inc(z_acc.sem[z], 1)
                    for z in range(LANES):
                        v.wait_ge(shifted.sem[z], shifted.at(i, 1, l))
                    halves = lambda z, tt: [Z[z][:, tt, 0:64], bank[z][2][:, tt * 64:(tt + 1) * 64]]
                    moments(halves)
                    for z in range(LANES):
                        normalise(z, XN, halves, 2 + l)
                    for z in range(LANES):
                        for c, (c0, w) in enumerate(CH):
                            v.wait_ge(up_mm.sem[z], up_mm.at(i, c + 1, l))
                            v.wait_ge(gelu.sem[z], gelu.at(i, c + 1, l))
                            v.scalar_tensor_tensor(out=G[z][0:w, c, :], in0=bank[z][c][0:w, :],
                                                   scalar=b1[0:w, l, 0, c:c + 1], in1=G[z][0:w, c, :],
                                                   op0=ALU.add, op1=ALU.mult).then_inc(hid.sem[z], 1)
                    for z in range(LANES):
                        v.wait_ge(down_mm.sem[z], down_mm.at(i, 1, l))
                        v.wait_ge(z_b2.sem[z], z_b2.at(i, 1, l))
                        zf = Z[z][:, :, :].rearrange("p t d -> p (t d)")
                        v.tensor_tensor(zf, bank[z][3], zf, ALU.add).then_inc(z_out.sem[z], 1)
                for z in range(LANES):
                    v.wait_ge(z_out.sem[z], z_out.at(i, 1, L - 1))
                    v.tensor_tensor(XN[z][:, :, :], X[z][:, :, :], Z[z][:, :, :], ALU.add).then_inc(fin.sem[z], 1)
            assert chain.count == DVE_ORDER, chain.count

        @block.scalar
        def _(a):
            a.wait_ge(consts, 16 * (N_CONST + L * 8))
            a.wait_ge(made, N_MADE)
            with a.Fori(0, PAIRS) as i:
                def to_xt(use, src_bank):
                    for z in range(LANES):
                        a.wait_ge(tr_done.sem[z], tr_done.at(i, 1, use))
                        a.copy(XT[z][:, :], bank[z][src_bank]).then_inc(xt_ready.sem[z], 1)

                to_xt(0, 3)
                for z in range(LANES):
                    a.wait_ge(v1_done.sem[z], v1_done.at(i, 1))
                    a.copy(V1[z][:, :, 0:H1 * VW].rearrange("p t (h e) -> p t h e", h=H1)[:, :, :, 0:E1],
                           bank[z][0].rearrange("p (t h e) -> p t h e", t=NT, h=H1)).then_inc(v1_ready.sem[z], 1)
                for z in range(LANES):
                    for w in range(2):
                        a.wait_ge(rope_sum.sem[z], rope_sum.at(i, w + 1))
                        a.copy(qkp[z][:, w, 0, :], rope_t[z][:, w, :]).then_inc(part_hi.sem[z], 1)
                for z in range(LANES):
                    for w in range(2):
                        a.wait_ge(part_res.sem[z], part_res.at(i, w + 1))
                        a.copy(qkp[z][:, w, 1, :], rope_s[z][:, w, :]).then_inc(part_mid.sem[z], 1)
                for z in range(LANES):
                    a.wait_ge(nm_tr.sem[z], nm_tr.at(i, 1))
                    a.copy(NMT[z], bank[z][3][:, 0:256].bitcast(BF16)).then_inc(nmt_ready.sem[z], 1)

                def evacuate(g):
                    for z in range(LANES):
                        a.wait_ge(pv_done.sem[z], pv_done.at(i, 2 * g + 2))
                        a.copy(U[z], bank[z][3]).then_inc(u_ready.sem[z], 1)

                for h in range(H1):
                    for z in range(LANES):
                        a.wait_ge(scored_t.sem[z], scored_t.at(i, h + 1))
                        if h >= 4:
                            a.wait_ge(pv_done.sem[z], pv_done.at(i, (h - 4) // 2 + 1))
                        a.activation(PT1[z][:, h % 4, :], region[z][:, 0:SCORES], ACT.Exp,
                                     scale=SCALE1).then_inc(exped.sem[z], 1)
                    if h % 4 == 0 and h >= 4:
                        evacuate(h // 4 - 1)
                evacuate(3)
                to_xt(1, 0)
                for l in range(L):
                    for z in range(LANES):
                        a.wait_ge(zt_tr.sem[z], zt_tr.at(i, 1, l))
                        a.copy(ZT[z][0:64, :], bank[z][0][0:64, :])
                        a.copy(ZT[z][64:128, 1:S], bank[z][0][64:128, 0:S - 1]).then_inc(zt_ready.sem[z], 1)
                    for tt in range(NT):
                        for z in range(LANES):
                            a.wait_ge(qk_done.sem[z], qk_done.at(i, tt + 1, l))
                            if tt:
                                a.wait_ge(ss_ready.sem[z], ss_ready.at(i, tt, l))
                            a.activation(SQ[z][:, 1, :], bank[z][1], ACT.Square).then_inc(k_squared.sem[z], 1)
                            a.wait_ge(q_rot.sem[z], q_rot.at(i, tt + 1, l))
                            a.activation(SQ[z][:, 0, :], bank[z][0], ACT.Square).then_inc(squared.sem[z], 1)
                            a.wait_ge(v_done.sem[z], v_done.at(i, tt + 1, l))
                            if tt:
                                a.wait_ge(pv2.sem[z], pv2.at(i, 2 * tt, l))
                            a.copy(V2[z], bank[z][2])
                            last64 = bank[z][2][64:128, :].rearrange("p (j s e) -> p j s e", j=PAIR2, s=2)
                            a.copy(VPB[z][64:128, tt % 2, :, 64:128], last64[:, :, 1, :])
                            a.copy(VPB[z][0:64, tt % 2, :, 0:64], last64[:, :, 0, :]).then_inc(v2_ready.sem[z], 1)
                        for z in range(LANES):
                            a.wait_ge(k_tr.sem[z], k_tr.at(i, tt + 1, l))
                            a.copy(KT[z][:, :, WIN + tt * P:WIN + (tt + 1) * P],
                                   bank[z][0].rearrange("p (j q) -> p j q", j=PAIR2)).then_inc(kt_ready.sem[z], 1)
                        for half in range(2):
                            u = 2 * tt + half + 1
                            for z in range(LANES):
                                a.wait_ge(nb2_ready.sem[z], nb2_ready.at(i, u, l))
                                if u > 1:
                                    a.wait_ge(p_ready.sem[z], p_ready.at(i, u - 1, l))
                                for n in range(4):
                                    h = 4 * half + n
                                    ins = a.activation(PR[z][:, n, :],
                                                       bank[z][1 + n // 2][:, (n % 2) * KEYS:(n % 2 + 1) * KEYS], ACT.Exp,
                                                       bias=nb2[z][:, n:n + 1], scale=inv[z][:, h:h + 1],
                                                       accum_out=sum2[z][:, n:n + 1])
                                ins.then_inc(exp2.sem[z], 1)
                            for z in range(LANES):
                                a.wait_ge(p_tr.sem[z], p_tr.at(i, u, l))
                                if u > 1:
                                    a.wait_ge(pv2.sem[z], pv2.at(i, u - 1, l))
                                a.copy(PTM[z], bank[z][3]).then_inc(ptm_ready.sem[z], 1)
                            for z in range(LANES):
                                a.wait_ge(pv2.sem[z], pv2.at(i, u, l))
                                if tt:
                                    a.wait_ge(wo2_done.sem[z], wo2_done.at(i, tt, l))
                                a.copy(OT[z][:, 2 * half:2 * half + 2, :],
                                       bank[z][0][:, 256:512].rearrange("p (j q) -> p j q", j=2)).then_inc(ot_ready.sem[z], 1)
                    for z in range(LANES):
                        a.wait_ge(tr_done.sem[z], tr_done.at(i, 1, 2 + l))
                        a.activation(XT[z][:, :], bank[z][0], ACT.Identity, scale=lgb[:, l, 0:1],
                                     bias=lgb[:, l, 1:2]).then_inc(xt_ready.sem[z], 1)
                    for z in range(LANES):
                        for c, (c0, w) in enumerate(CH):
                            a.wait_ge(gate_mm.sem[z], gate_mm.at(i, c + 1, l))
                            a.activation(G[z][0:w, c, :], bank[z][1 + c][0:w, :], ACT.Gelu,
                                         bias=b1[0:w, l, 1, c:c + 1]).then_inc(gelu.sem[z], 1)

        @block.gpsimd
        def _(g):
            for z in range(LANES):
                g.memset(XN[z][:, 0, 0:1], 0.0).then_inc(y_out[z].sem, 1)
                g.memset(V1[z][:, :, :], 1.0).then_inc(made, 1)
                g.memset(ZT[z][:, 0:1], 0.0).then_inc(made, 1)
                g.memset(nparts[z][:, :, :], 0.0).then_inc(made, 1)
                g.memset(QT[z][:, :, :, :], 0.0).then_inc(made, 1)
                g.memset(VPB[z][:, :, :, :], 0.0).then_inc(made, 1)
            g.memset(nhalf[:, :], -0.5).then_inc(made, 1)
            g.wait_ge(made, N_MADE)
            with g.Fori(0, PAIRS) as i:
                def root(z, use):
                    g.wait_ge(ln_var.sem[z], ln_var.at(i, 1, use))
                    g.tensor_tensor(rstd[z][:, :], veps[z][:, :], nhalf[:, 0:NT], ALU.pow).then_inc(ln_rstd.sem[z], 1)

                for z in range(LANES):
                    root(z, 0)
                for z in range(LANES):
                    root(z, 1)
                for l in range(L):
                    for tt in range(NT):
                        for z in range(LANES):
                            g.wait_ge(q_rot.sem[z], q_rot.at(i, tt + 1, l))
                            if tt:
                                g.wait_ge(k_tr.sem[z], k_tr.at(i, tt, l))
                            g.tensor_tensor(QR[z][:, 0, :], RC[z][:, 0, :], RS[z][:, 0, :], ALU.add).then_inc(q_ready.sem[z], 1)
                            g.wait_ge(rot_done.sem[z], rot_done.at(i, tt + 1, l))
                            g.tensor_tensor(RC[z][:, 1, :], RC[z][:, 1, :], RS[z][:, 1, :], ALU.add)
                            g.wait_ge(ss_ready.sem[z], ss_ready.at(i, tt + 1, l))
                            if tt:
                                g.wait_ge(exp2.sem[z], exp2.at(i, 2 * tt, l))
                            g.tensor_tensor(inv[z][:, :], ss[z][:, :], nhalf[:, :], ALU.pow).then_inc(inv_ready.sem[z], 1)
                            g.wait_ge(inv_ready.sem[z], inv_ready.at(i, tt + 1, l))
                            g.tensor_tensor(QR[z][:, 1, :].rearrange("p (h e) -> p h e", h=H2),
                                            RC[z][:, 1, :].rearrange("p (h e) -> p h e", h=H2),
                                            inv[z][:, H2:2 * H2].unsqueeze(2).to_broadcast([P, H2, E2]),
                                            ALU.mult).then_inc(k_ready.sem[z], 1)
                    for z in range(LANES):
                        root(z, 2 + l)
                    for z in range(LANES):
                        g.wait_ge(ln_out.sem[z], ln_out.at(i, 1, 2 + l))
                        g.tensor_tensor(Z[z][:, :, :], Z[z][:, :, :], b2[:, l:l + 1, :].to_broadcast([P, NT, D]),
                                        ALU.add).then_inc(z_b2.sem[z], 1)


def constants():
    f = np.float32
    bf = mybir.dt.np(BF16)
    q, k = np.arange(P)[:, None], np.arange(P)[None, :]
    c = np.arange(KEYS)[None, :]
    seen = (c >= q) & (c <= q + WIN)
    const = {
        "ident": np.eye(P, dtype=f), "identb": np.eye(P, dtype=bf),
        "causal": np.where(k > q, f(NEG), f(0)).astype(bf), "causal_t": np.where(q > k, f(NEG), f(0)).astype(bf),
        "band": np.where(seen, f(0), f(NEG)).astype(bf), "band0": np.where(seen & (c >= WIN), f(0), f(NEG)).astype(bf),
        "shift": np.eye(P, k=1, dtype=f), "corner": ((q == P - 1) & (k == 0)).astype(f),
        "ones": np.ones((SPLIT, H1 * S), bf),
    }
    freqs = (f(1.0) / f(10000.0) ** (np.arange(0, E1, 2, dtype=f) / f(E1))).astype(f)
    angle = np.arange(S, dtype=f)[:, None] * freqs[None, :]
    e = np.arange(P) // H1
    const["cos1"] = np.cos(angle).astype(f)[:, e // 2].T
    const["sin1"] = (np.sin(angle).astype(f)[:, e // 2] * np.where(e % 2, f(1), f(-1))).T
    half = np.arange(0, E2, 2, dtype=f)
    tok = np.arange(S, dtype=f)
    angle = tok[:, None] * (f(1.0) / f(10000.0) ** (half / f(E2)))[None, :]
    angle = np.concatenate([angle, angle], -1)
    base = (half + f(0.4 * E2)) / f(1.4 * E2)
    scale = base[None, :] ** ((tok - S // 2) / f(WIN // 2))[:, None]
    scale = np.concatenate([scale, scale], -1)
    sign = np.where(np.arange(E2) < E2 // 2, f(-1), f(1))
    cos, sin = np.cos(angle), np.sin(angle) * sign
    rot = np.stack([cos * scale * f(8), sin * scale * f(8), cos / scale, sin / scale])
    const["rot"] = rot.reshape(4, NT, P, E2).transpose(2, 0, 1, 3)
    return {n: np.ascontiguousarray(v, v.dtype if v.dtype == bf else f) for n, v in const.items()}


def kernel(**inputs):
    import concourse.bacc as bacc
    from concourse.bass_utils import run_bass_kernel_spmd as run

    a = {n.replace("L0_attn_", "a_").replace("L0_ffn_", "f_"): np.asarray(v) for n, v in inputs.items()}
    turned = np.arange(E1) ^ 1

    def by_width(w, order):
        return w.reshape(H1, E1, D)[:, order].transpose(2, 1, 0).reshape(D, D)

    same = np.arange(E1)
    swapped = np.roll(np.arange(E2), E2 // 2)
    b1 = np.zeros((P, L, 2, 3), a["f_b1"].dtype)
    for c, (c0, w) in enumerate(CH):
        for s in range(2):
            b1[0:w, :, s, c] = a["f_b1"][:, s * HID + c0:s * HID + c0 + w].T
    arrays = {
        "x": a["a_x"],
        "w1st": np.stack([by_width(a["a_wq"], same), by_width(a["a_wq"], turned), by_width(a["a_wk"], same),
                          by_width(a["a_wk"], turned), a["a_wv"].T, a["a_wo"].T], axis=1),
        "wqkv": a["f_wqkv"], "wo2": a["f_wo"], "w1": a["f_w1"], "w2": a["f_w2"], "b1": b1, "b2": a["f_b2"],
        "lgb": np.stack([a["f_ln_g"].T, a["f_ln_b"].T], axis=2),
        "scl": np.stack([a["f_q_scale"], a["f_q_scale"][:, swapped], a["f_k_scale"], a["f_k_scale"][:, swapped]], axis=1),
    }
    arrays.update(constants())
    arrays = {f"in_{n}": np.ascontiguousarray(v) for n, v in arrays.items()}
    nc = bacc.Bacc("TRN2", target_bir_lowering=False, num_devices=1)
    t = {n[3:]: nc.dram_tensor(n, v.shape, mybir.dt.from_np(v.dtype), kind="ExternalInput").ap()
         for n, v in arrays.items()}
    out = nc.dram_tensor("out", (B, S, D), F32, kind="ExternalOutput").ap()
    build(nc, t, out)
    return run(nc, [arrays], core_ids=[0]).results[0]["out"]
```

```python
from contextlib import ExitStack

import numpy as np

import concourse.bass as bass
from concourse import mybir

ALU = mybir.AluOpType
ACT = mybir.ActivationFunctionType
AX = mybir.AxisListType
F32 = mybir.dt.float32
BF16 = mybir.dt.bfloat16

P = 128
B, S, D = 16, 512, 128
NT = S // P
LANES = 2
PAIRS = B // LANES
EPS = 1e-5
H1, E1 = 16, 8
VW = E1 + 1
SPLIT = 3
QK_ROWS = SPLIT * SPLIT * E1
ROWS = QK_ROWS + SPLIT
SEG = {0: (0, 512), 1: (512, 384), 2: (1024, 256), 3: (896, 128)}
SCORES = 1280
SCALE1 = float(1.0 / np.sqrt(E1))
L = 2
H2, E2, WIN = 8, 64, 64
INNER = H2 * E2
PAIR2 = H2 // 2
KEYS = WIN + P
UNITS = NT * PAIR2
HID = int(D * 4 * 2 / 3)
CH = [(0, 128), (128, 128), (256, HID - 256)]
NEG = -3.0e38
DVE_ORDER = 174


class Next:

    def __init__(self, i):
        self.i = i

    def __mul__(self, n):
        return self.i * n + n


class Signal:

    def __init__(self, nc, ctx, name, n=1, uses=1):
        self.sem = [ctx.enter_context(nc.semaphore(f"{name}_{z}")) for z in range(LANES)]
        self.n, self.uses = n, uses

    def at(self, i, k=1, use=0):
        return i * (self.uses * self.n) + use * self.n + k


class Landed:

    def __init__(self, nc, ctx, name, n=1):
        self.sem = ctx.enter_context(nc.semaphore(name))
        self.n = n

    def before(self, i):
        return i * (16 * self.n)

    def now(self, i):
        return i * (16 * self.n) + 16 * self.n


class Chain:

    def __init__(self, nc, ctx, name, per_pair):
        self.sem = ctx.enter_context(nc.semaphore(name))
        self.per_pair, self.count = per_pair, 0

    def mark(self, ins):
        ins.then_inc(self.sem, 1)
        self.count += 1
        return self.count

    def wait(self, eng, i, mark):
        eng.wait_ge(self.sem, i * self.per_pair + mark)

    def link(self, eng, i, ins):
        self.wait(eng, i, self.mark(ins))


def build(nc, t, out):
    with ExitStack() as ctx:
        def sb(name, shape, dt=F32):
            return ctx.enter_context(nc.sbuf_tensor(name, shape, dt))

        def signal(name, n=1, uses=1):
            return Signal(nc, ctx, name, n, uses)

        def landed(name, n=1):
            return [Landed(nc, ctx, f"{name}{z}", n) for z in range(LANES)]

        ident = sb("ident", [P, P])
        identb = sb("identb", [P, P], BF16)
        causal = sb("causal", [P, P], BF16)
        causal_t = sb("causal_t", [P, P], BF16)
        band = sb("band", [P, KEYS], BF16)
        band0 = sb("band0", [P, KEYS], BF16)
        shift = sb("shift", [P, P])
        corner = sb("corner", [P, P])
        cos1 = sb("cos1", [P, S])
        sin1 = sb("sin1", [P, S])
        w1st = sb("w1st", [P, 6, P])
        rot = sb("rot", [P, L, 4, NT, E2])
        scl = sb("scl", [P, L, 4, E2])
        wqkv = sb("wqkv", [P, L, 3 * INNER])
        wo2 = sb("wo2", [P, L, PAIR2, D])
        w1 = sb("w1", [P, L, 2 * HID])
        w2 = sb("w2", [P, L, 3, D])
        b1 = sb("b1", [P, L, 2, 3])
        b2 = sb("b2", [P, L, D])
        lgb = sb("lgb", [P, L, 2])
        nhalf = sb("nhalf", [P, 2 * H2])
        X = [sb(f"X{z}", [P, NT, D]) for z in range(LANES)]
        Z = [sb(f"Z{z}", [P, NT, D]) for z in range(LANES)]
        XN = [sb(f"XN{z}", [P, NT, D]) for z in range(LANES)]
        ZT = [sb(f"ZT{z}", [P, S]) for z in range(LANES)]
        stats = [sb(f"stats{z}", [P, NT, 12]) for z in range(LANES)]
        stats_next = [sb(f"stats_next{z}", [P, NT, 12]) for z in range(LANES)]
        mv = [sb(f"mv{z}", [P, NT, 2]) for z in range(LANES)]
        mv_next = [sb(f"mv_next{z}", [P, NT, 2]) for z in range(LANES)]
        veps = [sb(f"veps{z}", [P, NT]) for z in range(LANES)]
        veps_next = [sb(f"veps_next{z}", [P, NT]) for z in range(LANES)]
        rstd = [sb(f"rstd{z}", [P, NT]) for z in range(LANES)]
        rstd_next = [sb(f"rstd_next{z}", [P, NT]) for z in range(LANES)]
        nmax = [sb(f"nmax{z}", [P, NT, H1]) for z in range(LANES)]
        nres = [sb(f"nres{z}", [P, NT, H1]) for z in range(LANES)]
        nparts = [sb(f"nparts{z}", [P, NT, P], BF16) for z in range(LANES)]
        rec1 = [sb(f"rec1{z}", [P, NT, 4]) for z in range(LANES)]
        V1 = [sb(f"V1{z}", [P, NT, H1 * VW + 32 - VW]) for z in range(LANES)]
        mix = [sb(f"mix{z}", [P, 1536]) for z in range(LANES)]
        qkp = [m[:, :].bitcast(BF16).rearrange("p (w a s) -> p w a s", w=2, a=SPLIT) for m in mix]
        X_next = [m[:, 0:512].rearrange("p (t d) -> p t d", t=NT) for m in mix]
        U = [m[:, 0:512] for m in mix]
        MG = [m[:, 512:1024].rearrange("p (t c) -> p t c", t=NT) for m in mix]
        NMT = [m[:, 1024:1280].bitcast(BF16) for m in mix]
        QT = [sb(f"QT{z}", [P, 2, PAIR2, P]) for z in range(LANES)]
        VPB = [sb(f"VPB{z}", [P, 3, PAIR2, P]) for z in range(LANES)]
        ss = [sb(f"ss{z}", [P, 2 * H2]) for z in range(LANES)]
        inv = [sb(f"inv{z}", [P, 2, 2 * H2]) for z in range(LANES)]
        nm2 = [sb(f"nm2{z}", [P, 4]) for z in range(LANES)]
        nb2 = [sb(f"nb2{z}", [P, 4]) for z in range(LANES)]
        sum2 = [sb(f"sum2{z}", [P, 4]) for z in range(LANES)]
        rec2 = [sb(f"rec2{z}", [P, 4]) for z in range(LANES)]
        arr = [sb(f"arr{z}", [P, 8192]) for z in range(LANES)]
        QA = [a[:, 0:4096].bitcast(BF16).rearrange("p (h s) -> p h s", h=H1) for a in arr]
        KA = [a[:, 4096:8192].bitcast(BF16).rearrange("p (h s) -> p h s", h=H1) for a in arr]
        SQ = [a[:, 0:1024].rearrange("p (w c) -> p w c", w=2) for a in arr]
        RC = [a[:, 1024:2048].rearrange("p (w c) -> p w c", w=2) for a in arr]
        RS = [a[:, 2048:3072].rearrange("p (w c) -> p w c", w=2) for a in arr]
        QR = [a[:, 3072:4096].rearrange("p (w c) -> p w c", w=2) for a in arr]
        PR = [a[:, 4096:4864].rearrange("p (b h c) -> p b h c", b=2, h=2) for a in arr]
        PM = [a[:, 6144:6656].rearrange("p (b c) -> p b c", b=2) for a in arr]
        PP = [a[:, 6656:6912].rearrange("p (b c) -> p b c", b=2) for a in arr]
        PT = [a[:, 4864:5632].rearrange("p (b c) -> p b c", b=2) for a in arr]
        OT = [a[:, 5632:6144].rearrange("p (j q) -> p j q", j=PAIR2) for a in arr]
        rope_t = [a[:, 0:1024].rearrange("p (w c) -> p w c", w=2) for a in arr]
        rope_s = [a[:, 1024:2048].rearrange("p (w c) -> p w c", w=2) for a in arr]
        prob = [sb(f"prob{z}", [P, 4 * SCORES]) for z in range(LANES)]
        PT1 = [p[:, :].rearrange("p (b c) -> p b c", b=4) for p in prob]
        KT = [p[:, 0:PAIR2 * (WIN + S)].rearrange("p (j s) -> p j s", j=PAIR2) for p in prob]
        V2 = [p[:, 2304:3328].rearrange("p (b c) -> p b c", b=2) for p in prob]
        XT = [p[:, 4608:5120] for p in prob]
        G = [p[:, 2048:2048 + 3 * S].rearrange("p (c s) -> p c s", c=3) for p in prob]
        XN_next = [p[:, 3584:4096].rearrange("p (t d) -> p t d", t=NT) for p in prob]
        XT_next = [p[:, 4096:4608] for p in prob]

        ps = ctx.enter_context(nc.psum_tensor("ps", [P, 8, 512], F32))
        bank = [[ps[:, 4 * z + n, :] for n in range(4)] for z in range(LANES)]
        region = [ps[:, 4 * z:4 * z + 3, :].rearrange("p b c -> p (b c)") for z in range(LANES)]
        parts_dram = [nc.dram_tensor(f"parts{z}", (2, SPLIT * E1, H1 * S), BF16, kind="Internal").ap()
                      for z in range(LANES)]

        consts = ctx.enter_context(nc.semaphore("consts"))
        made = ctx.enter_context(nc.semaphore("made"))
        tables = ctx.enter_context(nc.semaphore("tables"))
        x_in = landed("x_in")
        x_next_in = landed("x_next_in")
        next_var = signal("next_var")
        next_rstd = signal("next_rstd")
        next_ln = signal("next_ln")
        next_tr = signal("next_tr")
        next_xt = signal("next_xt")
        ln_var = signal("ln_var", uses=1 + L)
        ln_rstd = signal("ln_rstd", uses=1 + L)
        ln_out = signal("ln_out", uses=1 + L)
        tr_done = signal("tr_done", uses=1 + L)
        xt_ready = signal("xt_ready", uses=1 + L)
        proj = signal("proj", n=2)
        v1_done = signal("v1_done")
        v1_ready = signal("v1_ready")
        roped = signal("roped", n=2)
        rope_sum = signal("rope_sum", n=2)
        part_hi = signal("part_hi", n=2)
        part_res = signal("part_res", n=2)
        part_mid = signal("part_mid", n=2)
        parts = signal("parts", n=2)
        stored = [landed("stored_q"), landed("stored_k")]
        laid = landed("laid", 2 * SPLIT + 1)
        scored = signal("scored", n=H1)
        maxed = signal("maxed", n=H1)
        nm_parts = signal("nm_parts")
        nm_tr = signal("nm_tr")
        nmt_ready = signal("nmt_ready")
        nm_laid = landed("nm_laid", SPLIT)
        scored_t = signal("scored_t", n=H1)
        exped = signal("exped", n=H1)
        pv_done = signal("pv_done", n=H1 // 2)
        u_ready = signal("u_ready", n=4)
        u_tr = signal("u_tr", n=4)
        mg_ready = signal("mg_ready", n=4)
        wo_done = signal("wo_done")
        x1_ready = signal("x1_ready")
        zt_tr = signal("zt_tr", uses=L)
        zt_ready = signal("zt_ready", uses=L)
        qk_done = signal("qk_done", n=NT, uses=L)
        v_done = signal("v_done", n=NT, uses=L)
        k_squared = signal("k_squared", n=NT, uses=L)
        squared = signal("squared", n=NT, uses=L)
        q_rot = signal("q_rot", n=NT, uses=L)
        rot_done = signal("rot_done", n=NT, uses=L)
        ss_ready = signal("ss_ready", n=NT, uses=L)
        inv_ready = signal("inv_ready", n=NT, uses=L)
        q_ready = signal("q_ready", n=NT, uses=L)
        k_ready = signal("k_ready", n=NT, uses=L)
        q_tr = signal("q_tr", n=NT, uses=L)
        k_tr = signal("k_tr", n=NT, uses=L)
        qt_ready = signal("qt_ready", n=NT, uses=L)
        kt_ready = signal("kt_ready", n=NT, uses=L)
        pad_ready = signal("pad_ready", uses=L)
        v2_ready = signal("v2_ready", n=NT, uses=L)
        s2_done = signal("s2_done", n=UNITS, uses=L)
        nb2_ready = signal("nb2_ready", n=UNITS, uses=L)
        exp2 = signal("exp2", n=UNITS, uses=L)
        p_ready = signal("p_ready", n=UNITS, uses=L)
        p_tr = signal("p_tr", n=UNITS, uses=L)
        pt_ready = signal("pt_ready", n=UNITS, uses=L)
        pv2 = signal("pv2", n=UNITS, uses=L)
        ot_ready = signal("ot_ready", n=UNITS, uses=L)
        wo2_done = signal("wo2_done", n=NT, uses=L)
        z_acc = signal("z_acc", n=NT, uses=L)
        shifted = signal("shifted", uses=L)
        z_b2 = signal("z_b2", uses=L)
        gate_mm = signal("gate_mm", n=3, uses=L)
        gelu = signal("gelu", n=3, uses=L)
        up_mm = signal("up_mm", n=3, uses=L)
        hid = signal("hid", n=3, uses=L)
        down_mm = signal("down_mm", uses=L)
        z_out = signal("z_out", uses=L)
        fin = signal("fin")
        y_out = landed("y_out")
        N_CONST = 17
        N_MADE = 5 * LANES + 1

        block = ctx.enter_context(nc.Block())

        @block.sync
        def _(sp):
            for dst, src in (
                (w1st[:, :, :], t["w1st"]), (ident[:, :], t["ident"]), (identb[:, :], t["identb"]),
                (cos1[:, :], t["cos1"]), (sin1[:, :], t["sin1"]), (causal[:, :], t["causal"]),
                (causal_t[:, :], t["causal_t"]), (band[:, :], t["band"]), (band0[:, :], t["band0"]),
                (shift[:, :], t["shift"]), (corner[:, :], t["corner"]),
                (wqkv[:, :, :], t["wqkv"].rearrange("l d n -> d l n")),
                (wo2[:, :, :, :], t["wo2"].rearrange("l (j p) n -> p l j n", p=P)),
                (w1[:, :, :], t["w1"].rearrange("l d n -> d l n")),
                (b2[:, :, :], t["b2"].rearrange("(o l) n -> o l n", o=1).to_broadcast([P, L, D])),
                (lgb[:, :, :], t["lgb"]),
                (b1[:, :, :, :], t["b1"]),
            ):
                sp.dma_start(dst, src).then_inc(consts, 16)
            for l in range(L):
                for c, (c0, w) in enumerate(CH):
                    sp.dma_start(w2[0:w, l, c, :], t["w2"][l, c0:c0 + w, :]).then_inc(consts, 16)
                sp.dma_start(rot[:, l, :, :, :], t["rot"]).then_inc(consts, 16)
                for n in range(4):
                    sp.dma_start(scl[:, l, n, :],
                                 t["scl"][l:l + 1, n, :].to_broadcast([P, E2])).then_inc(consts, 16)

            def load_next(batches):
                for z in range(LANES):
                    sp.dma_start(X_next[z], t["x"][batches[z]].rearrange("(t p) d -> p t d", p=P)).then_inc(
                        x_next_in[z].sem, 16)

            def lay_out(n):
                for z in range(LANES):
                    for w in range(2):
                        sp.wait_ge(parts.sem[z], parts.at(n, w + 1))
                        sp.dma_start(parts_dram[z][w].rearrange("(a p) (h s) -> (p h) a s", a=SPLIT, h=H1),
                                     qkp[z][:, w, :, :]).then_inc(stored[w][z].sem, 16)
                for z in range(LANES):
                    for w in range(2):
                        sp.wait_ge(stored[w][z].sem, stored[w][z].now(n))
                        for a in range(SPLIT):
                            r0 = a * SPLIT * E1
                            if w == 0:
                                src = parts_dram[z][0, a * E1:(a + 1) * E1, :]
                                src = src.rearrange("(o p) c -> o p c", o=1).to_broadcast([SPLIT, E1, H1 * S])
                                dst = QA[z][r0:r0 + SPLIT * E1, :, :]
                            else:
                                src = parts_dram[z][1]
                                dst = KA[z][r0:r0 + SPLIT * E1, :, :]
                            sp.dma_start(dst, src).then_inc(laid[z].sem, 16)
                    sp.dma_start(KA[z][QK_ROWS:ROWS, :, :], t["ones"]).then_inc(laid[z].sem, 16)

            load_next(list(range(LANES)))
            lay_out(0)
            with sp.Fori(0, PAIRS) as i:
                row = [sp.snap(i * LANES + z) for z in range(2 * LANES)]
                for z in range(LANES):
                    sp.dma_start(X[z][:, :, :],
                                 t["x"][row[z]].rearrange("(t p) d -> p t d", p=P)).then_inc(x_in[z].sem, 16)
                for z in range(LANES):
                    sp.wait_ge(nmt_ready.sem[z], nmt_ready.at(i, 1))
                    for a in range(SPLIT):
                        sp.dma_start(QA[z][QK_ROWS + a:QK_ROWS + a + 1, :, :],
                                     NMT[z][a * H1:(a + 1) * H1, :]).then_inc(nm_laid[z].sem, 16)
                for z in range(LANES):
                    sp.wait_ge(x1_ready.sem[z], x1_ready.at(i, 1))
                load_next(row[LANES:])
                lay_out(Next(i))
                for z in range(LANES):
                    batch = row[z]
                    sp.wait_ge(fin.sem[z], fin.at(i, 1))
                    sp.dma_start(out[batch].rearrange("(t p) d -> p t d", p=P),
                                 XN[z][:, :, :]).then_inc(y_out[z].sem, 16)
            for z in range(LANES):
                sp.wait_ge(y_out[z].sem, 1 + 16 * PAIRS)
                sp.wait_ge(laid[z].sem, laid[z].now(PAIRS))

        @block.tensor
        def _(pe):
            pe.wait_ge(consts, 16 * (N_CONST + L * 8))
            pe.wait_ge(made, N_MADE)

            def turn(dst, src, n=NT):
                for tt in range(n):
                    last = pe.transpose(dst[:, tt * P:(tt + 1) * P], src(tt), ident[:, :])
                return last

            def next_turn(n):
                for z in range(LANES):
                    pe.wait_ge(next_ln.sem[z], next_ln.at(n, 1))
                    turn(bank[z][0], lambda tt: XN_next[z][:, tt, :]).then_inc(next_tr.sem[z], 1)

            def next_project(n, w):
                for z in range(LANES):
                    if w:
                        pe.wait_ge(roped.sem[z], roped.at(n, 1))
                    else:
                        pe.wait_ge(next_xt.sem[z], next_xt.at(n, 1))
                    for m in range(2):
                        mm = pe.matmul(bank[z][m], w1st[:, 2 * w + m, :], XT_next[z], start=True, stop=True)
                    mm.then_inc(proj.sem[z], 1)

            def next_values(n):
                for z in range(LANES):
                    pe.wait_ge(roped.sem[z], roped.at(n, 2))
                    for tt in range(NT):
                        mm = pe.matmul(bank[z][0][:, tt * P:(tt + 1) * P], XT_next[z][:, tt * P:(tt + 1) * P],
                                       w1st[:, 4, :], start=True, stop=True)
                    mm.then_inc(v1_done.sem[z], 1)

            next_turn(0)
            next_project(0, 0)
            next_project(0, 1)
            next_values(0)
            with pe.Fori(0, PAIRS) as i:
                for h in range(H1):
                    for z in range(LANES):
                        if h == 0:
                            pe.wait_ge(v1_ready.sem[z], v1_ready.at(i, 1))
                            pe.wait_ge(laid[z].sem, laid[z].now(i))
                        else:
                            pe.wait_ge(maxed.sem[z], maxed.at(i, h))
                        for r in range(NT):
                            qt = NT - 1 - r
                            c0, w = SEG[r]
                            pe.matmul(region[z][:, c0:c0 + w], QA[z][0:QK_ROWS, h, qt * P:(qt + 1) * P],
                                      KA[z][0:QK_ROWS, h, 0:w], start=True, stop=False)
                            last = pe.matmul(region[z][:, c0 + w - P:c0 + w], identb[:, :], causal[:, :],
                                             start=False, stop=True)
                        last.then_inc(scored.sem[z], 1)
                for z in range(LANES):
                    pe.wait_ge(nm_parts.sem[z], nm_parts.at(i, 1))
                    tp = bank[z][3][:, 0:256].bitcast(BF16)
                    for tt in range(NT):
                        last = pe.transpose(tp[:, tt * P:(tt + 1) * P],
                                            nparts[z][:, tt, :], identb[:, :])
                    last.then_inc(nm_tr.sem[z], 1)

                def values(j):
                    for z in range(LANES):
                        if j == 0:
                            pe.wait_ge(nmt_ready.sem[z], nmt_ready.at(i, 1))
                        elif j % 2 == 0:
                            pe.wait_ge(mg_ready.sem[z], mg_ready.at(i, j // 2))
                        pe.wait_ge(exped.sem[z], exped.at(i, 2 * j + 2))
                    for kt in range(NT):
                        c0, w = SEG[kt]
                        for z in range(LANES):
                            for s in range(2):
                                h = 2 * j + s
                                q0 = 32 * ((h + 2 * z) % 4)
                                last = pe.matmul(bank[z][3][q0:q0 + 32, kt * P:S],
                                                 V1[z][:, kt, h * VW:h * VW + 32],
                                                 PT1[z][:, h % 4, c0:c0 + w], start=(kt == 0), stop=(kt == NT - 1))
                            if kt == NT - 1:
                                last.then_inc(pv_done.sem[z], 1)

                def heads_out(g):
                    for z in range(LANES):
                        pe.wait_ge(u_ready.sem[z], u_ready.at(i, g + 1))
                        turn(bank[z][3], lambda tt: U[z][:, tt * P:(tt + 1) * P]).then_inc(u_tr.sem[z], 1)

                for h in range(H1):
                    for z in range(LANES):
                        if h == 0:
                            pe.wait_ge(maxed.sem[z], maxed.at(i, H1))
                            pe.wait_ge(nm_laid[z].sem, nm_laid[z].now(i))
                        else:
                            pe.wait_ge(exped.sem[z], exped.at(i, h))
                        for kt in range(NT):
                            c0, w = SEG[kt]
                            pe.matmul(region[z][:, c0:c0 + w], KA[z][0:ROWS, h, kt * P:(kt + 1) * P],
                                      QA[z][0:ROWS, h, kt * P:S], start=True, stop=False)
                            last = pe.matmul(region[z][:, c0:c0 + P], identb[:, :], causal_t[:, :],
                                             start=False, stop=True)
                        last.then_inc(scored_t.sem[z], 1)
                    if h % 2 == 0 and h >= 2:
                        values(h // 2 - 1)
                    if h % 4 == 1 and h >= 5:
                        heads_out(h // 4 - 1)
                values(H1 // 2 - 1)
                heads_out(3)
                for z in range(LANES):
                    pe.wait_ge(mg_ready.sem[z], mg_ready.at(i, 4))
                    pe.wait_ge(exped.sem[z], exped.at(i, H1))
                    turn(bank[z][0], lambda tt: MG[z][:, tt, :]).then_inc(tr_done.sem[z], 1)
                for z in range(LANES):
                    pe.wait_ge(xt_ready.sem[z], xt_ready.at(i, 1, 0))
                    for tt in range(NT):
                        last = pe.matmul(bank[z][1][:, tt * P:(tt + 1) * P], XT[z][:, tt * P:(tt + 1) * P],
                                         w1st[:, 5, :], start=True, stop=True)
                    last.then_inc(wo_done.sem[z], 1)

                def project_qk(l, tt):
                    for z in range(LANES):
                        if tt == 0:
                            pe.wait_ge(zt_ready.sem[z], zt_ready.at(i, 1, l))
                        else:
                            pe.wait_ge(kt_ready.sem[z], kt_ready.at(i, tt, l))
                            pe.wait_ge(qt_ready.sem[z], qt_ready.at(i, tt, l))
                        for n in range(2):
                            mm = pe.matmul(bank[z][n], ZT[z][:, tt * P:(tt + 1) * P],
                                           wqkv[:, l, n * INNER:(n + 1) * INNER], start=True, stop=True)
                        mm.then_inc(qk_done.sem[z], 1)

                def project_v(l, tt):
                    for z in range(LANES):
                        pe.wait_ge(q_rot.sem[z], q_rot.at(i, tt + 1, l))
                        pe.wait_ge(squared.sem[z], squared.at(i, tt + 1, l))
                        pe.matmul(bank[z][0], ZT[z][:, tt * P:(tt + 1) * P], wqkv[:, l, 2 * INNER:3 * INNER],
                                  start=True, stop=True).then_inc(v_done.sem[z], 1)

                def turn_q(l, tt):
                    for z in range(LANES):
                        pe.wait_ge(q_ready.sem[z], q_ready.at(i, tt + 1, l))
                        pe.wait_ge(rot_done.sem[z], rot_done.at(i, tt + 1, l))
                        if tt >= 2:
                            pe.wait_ge(z_acc.sem[z], z_acc.at(i, tt - 1, l))
                        turn(bank[z][1], lambda j: QR[z][:, 0, j * P:(j + 1) * P]).then_inc(q_tr.sem[z], 1)

                def turn_k(l, tt):
                    for z in range(LANES):
                        pe.wait_ge(k_ready.sem[z], k_ready.at(i, tt + 1, l))
                        pe.wait_ge(v2_ready.sem[z], v2_ready.at(i, tt + 1, l))
                        turn(bank[z][0], lambda j: QR[z][:, 1, j * P:(j + 1) * P]).then_inc(k_tr.sem[z], 1)

                def scores(l, u):
                    tt, j = u // PAIR2, u % PAIR2
                    for z in range(LANES):
                        if j == 0:
                            pe.wait_ge(qt_ready.sem[z], qt_ready.at(i, tt + 1, l))
                            pe.wait_ge(kt_ready.sem[z], kt_ready.at(i, tt + 1, l))
                        if u == 0:
                            pe.wait_ge(pad_ready.sem[z], pad_ready.at(i, 1, l))
                        else:
                            pe.wait_ge(exp2.sem[z], exp2.at(i, u, l))
                        for s in range(2):
                            dst = bank[z][2][:, s * KEYS:(s + 1) * KEYS]
                            pe.matmul(dst, QT[z][:, s, j, :], KT[z][:, j, tt * P:tt * P + KEYS],
                                      start=True, stop=False)
                            mm = pe.matmul(dst, identb[:, :], (band if tt else band0)[:, :],
                                           start=False, stop=True)
                        mm.then_inc(s2_done.sem[z], 1)

                def turn_p(l, u):
                    for z in range(LANES):
                        pe.wait_ge(p_ready.sem[z], p_ready.at(i, u + 1, l))
                        if u >= 2:
                            pe.wait_ge(ot_ready.sem[z], ot_ready.at(i, u - 1, l))
                        elif u == 1:
                            pe.wait_ge(pt_ready.sem[z], pt_ready.at(i, u, l))
                        for s in range(2):
                            mm = pe.transpose(bank[z][3][:, s * P:(s + 1) * P], PM[z][:, u % 2, s * P:(s + 1) * P],
                                              ident[:, :])
                        if u >= PAIR2:
                            mm = pe.transpose(bank[z][3][:, 2 * P:3 * P], PP[z][:, u % 2, :], ident[:, :])
                        mm.then_inc(p_tr.sem[z], 1)

                def attend(l, u):
                    tt, j = u // PAIR2, u % PAIR2
                    for z in range(LANES):
                        pe.wait_ge(pt_ready.sem[z], pt_ready.at(i, u + 1, l))
                        if u == UNITS - 1:
                            pe.wait_ge(ot_ready.sem[z], ot_ready.at(i, u, l))
                        dst = bank[z][3][:, 3 * P:4 * P]
                        for s in range(2):
                            mm = pe.matmul(dst[s * E2:(s + 1) * E2, :],
                                           V2[z][:, tt % 2, (2 * j + s) * E2:(2 * j + s + 1) * E2],
                                           PT[z][:, u % 2, s * P:(s + 1) * P], start=True, stop=(tt == 0))
                        if tt:
                            mm = pe.matmul(dst, VPB[z][:, (tt - 1) % 3, j, :], PT[z][:, u % 2, 2 * P:3 * P],
                                           start=False, stop=True)
                        mm.then_inc(pv2.sem[z], 1)

                def merge(l, tt):
                    for z in range(LANES):
                        pe.wait_ge(ot_ready.sem[z], ot_ready.at(i, PAIR2 * (tt + 1), l))
                        if tt + 2 < NT:
                            pe.wait_ge(rot_done.sem[z], rot_done.at(i, tt + 3, l))
                        for j in range(PAIR2):
                            mm = pe.matmul(bank[z][1][:, 0:D], OT[z][:, j, :], wo2[:, l, j, :],
                                           start=(j == 0), stop=(j == PAIR2 - 1))
                        mm.then_inc(wo2_done.sem[z], 1)

                for l in range(L):
                    for z in range(LANES):
                        if l == 0:
                            pe.wait_ge(ln_out.sem[z], ln_out.at(i, 1, 0))
                        else:
                            pe.wait_ge(z_out.sem[z], z_out.at(i, 1, l - 1))
                        turn(bank[z][0], lambda tt: Z[z][:, tt, :]).then_inc(zt_tr.sem[z], 1)
                    project_qk(l, 0)
                    project_v(l, 0)
                    turn_q(l, 0)
                    turn_k(l, 0)
                    for tt in range(NT):
                        for k in range(PAIR2):
                            u = tt * PAIR2 + k
                            scores(l, u)
                            if k == 0 and tt < NT - 1:
                                project_qk(l, tt + 1)
                            if k == 3 and tt < NT - 1:
                                turn_q(l, tt + 1)
                            if u >= 1:
                                turn_p(l, u - 1)
                            if k == 2 and tt < NT - 1:
                                project_v(l, tt + 1)
                            if u >= 2:
                                attend(l, u - 2)
                            if k == 2 and tt >= 1:
                                if l == L - 1 and tt == NT - 1:
                                    for z in range(LANES):
                                        pe.wait_ge(roped.sem[z], roped.at(Next(i), 1))
                                merge(l, tt - 1)
                            if k == 3 and tt < NT - 1:
                                turn_k(l, tt + 1)
                            if l == L - 1 and tt == NT - 1:
                                if k == 0:
                                    next_turn(Next(i))
                                if k == 1:
                                    next_project(Next(i), 0)
                                if k == 3:
                                    for z in range(LANES):
                                        pe.wait_ge(z_acc.sem[z], z_acc.at(i, NT - 1, l))
                                    next_project(Next(i), 1)
                    turn_p(l, UNITS - 1)
                    attend(l, UNITS - 2)
                    attend(l, UNITS - 1)
                    if l == L - 1:
                        next_values(Next(i))
                    merge(l, NT - 1)
                    for z in range(LANES):
                        pe.wait_ge(z_acc.sem[z], z_acc.at(i, NT, l))
                        pe.matmul(bank[z][2][:, 0:NT * 64], shift[:, :], Z[z][:, :, 64:128], start=True, stop=True)
                        pe.matmul(bank[z][2][:, 64:NT * 64], corner[:, :], Z[z][:, 0:NT - 1, 64:128], start=False,
                                  stop=True, skip_group_check=True).then_inc(shifted.sem[z], 1)
                    for z in range(LANES):
                        pe.wait_ge(ln_out.sem[z], ln_out.at(i, 1, 1 + l))
                        if l == L - 1:
                            pe.wait_ge(v1_ready.sem[z], v1_ready.at(Next(i), 1))
                        turn(bank[z][0], lambda tt: XN[z][:, tt, :]).then_inc(tr_done.sem[z], 1)
                    for z in range(LANES):
                        pe.wait_ge(xt_ready.sem[z], xt_ready.at(i, 1, 1 + l))
                        for c, (c0, w) in enumerate(CH):
                            pe.matmul(bank[z][1 + c][0:w, :], w1[:, l, HID + c0:HID + c0 + w], XT[z],
                                      start=True, stop=True).then_inc(gate_mm.sem[z], 1)
                    for z in range(LANES):
                        for c, (c0, w) in enumerate(CH):
                            if c:
                                pe.wait_ge(gelu.sem[z], gelu.at(i, c, l))
                            pe.matmul(bank[z][c][0:w, :], w1[:, l, c0:c0 + w], XT[z],
                                      start=True, stop=True).then_inc(up_mm.sem[z], 1)
                    for z in range(LANES):
                        pe.wait_ge(hid.sem[z], hid.at(i, 3, l))
                        for tt in range(NT):
                            for c, (c0, w) in enumerate(CH):
                                mm = pe.matmul(bank[z][3][:, tt * P:(tt + 1) * P], G[z][0:w, c, tt * P:(tt + 1) * P],
                                               w2[0:w, l, c, :], start=(c == 0), stop=(c == 2))
                        mm.then_inc(down_mm.sem[z], 1)

        @block.vector
        def _(v):
            v.wait_ge(consts, 16 * (N_CONST + L * 8))
            for l in range(L):
                for n in range(4):
                    m = v.tensor_tensor(rot[:, l, n, :, :], rot[:, l, n, :, :],
                                        scl[:, l, n:n + 1, :].to_broadcast([P, NT, E2]), ALU.mult)
            m.then_inc(tables, 1)
            v.wait_ge(tables, 1)
            v.wait_ge(made, N_MADE)
            chain = Chain(nc, ctx, "dve_order", DVE_ORDER)

            this = (stats, mv, veps, rstd), ln_var, ln_rstd, ln_out
            following = (stats_next, mv_next, veps_next, rstd_next), next_var, next_rstd, next_ln

            def moments(i, pieces, which):
                (stats, mv, veps, _), var, _, _ = which
                counted = []
                for z in range(LANES):
                    for tt in range(NT):
                        n = len(pieces(z, tt))
                        for m, piece in enumerate(pieces(z, tt)):
                            if z == 1 and tt == NT - 1 and m == n - 1:
                                chain.wait(v, i, counted[0])
                            ins = v.bn_stats(stats[z][:, tt, 6 * m:6 * m + 6], piece)
                    counted.append(chain.mark(ins))
                for z in range(LANES):
                    for tt in range(NT):
                        ins = v.bn_aggr(mv[z][:, tt, :], stats[z][:, tt, 0:6 * n])
                    chain.link(v, i, ins)
                    if z == 0:
                        chain.wait(v, i, counted[1])
                    v.tensor_scalar(veps[z][:, :], mv[z][:, :, 1], EPS, None, ALU.add).then_inc(var.sem[z], 1)

            def normalise(n, z, dst, pieces, which, use=0):
                (_, mv, _, rstd), _, root, done = which
                v.wait_ge(root.sem[z], root.at(n, 1, use))
                for tt in range(NT):
                    c = 0
                    for piece in pieces(z, tt):
                        w = piece.shape[-1]
                        ins = v.tensor_scalar(dst[z][:, tt, c:c + w], piece, mv[z][:, tt, 0:1],
                                              rstd[z][:, tt:tt + 1], ALU.subtract, ALU.mult)
                        c += w
                ins.then_inc(done.sem[z], 1)

            next_x = lambda z, tt: [X_next[z][:, tt, :]]

            def next_moments(n, i):
                for z in range(LANES):
                    v.wait_ge(x_next_in[z].sem, x_next_in[z].now(n))
                moments(i, next_x, following)

            def next_normalise(n):
                for z in range(LANES):
                    normalise(n, z, XN_next, next_x, following)

            def next_rope(n, w):
                for z in range(LANES):
                    v.wait_ge(proj.sem[z], proj.at(n, w + 1))
                    v.tensor_tensor(rope_t[z][:, w, :], bank[z][0], cos1[:, :], ALU.mult)
                    v.tensor_tensor(rope_s[z][:, w, :], bank[z][1], sin1[:, :],
                                    ALU.mult).then_inc(roped.sem[z], 1)

            def next_sum(n, w):
                for z in range(LANES):
                    v.wait_ge(roped.sem[z], roped.at(n, w + 1))
                    v.tensor_tensor(rope_t[z][:, w, :], rope_t[z][:, w, :], rope_s[z][:, w, :],
                                    ALU.add).then_inc(rope_sum.sem[z], 1)

            def next_rest(n, w):
                for z in range(LANES):
                    v.wait_ge(part_hi.sem[z], part_hi.at(n, w + 1))
                    v.tensor_tensor(rope_s[z][:, w, :], rope_t[z][:, w, :], qkp[z][:, w, 0, :],
                                    ALU.subtract).then_inc(part_res.sem[z], 1)

            def next_low(n, w):
                for z in range(LANES):
                    v.wait_ge(part_mid.sem[z], part_mid.at(n, w + 1))
                    v.tensor_tensor(qkp[z][:, w, 2, :], rope_s[z][:, w, :], qkp[z][:, w, 1, :],
                                    ALU.subtract).then_inc(parts.sem[z], 1)

            next_moments(0, 0)
            next_normalise(0)
            for step in (next_rope, next_sum, next_rest, next_low):
                for w in range(2):
                    step(0, w)
            before_loop = chain.count

            with v.Fori(0, PAIRS) as i:
                for h in range(H1):
                    for z in range(LANES):
                        v.wait_ge(scored.sem[z], scored.at(i, h + 1))
                        for r in range(NT):
                            c0, w = SEG[r]
                            ins = v.tensor_reduce(nmax[z][:, NT - 1 - r, h:h + 1], region[z][:, c0:c0 + w], AX.X,
                                                  ALU.max, negate=True)
                        ins.then_inc(maxed.sem[z], 1)
                for z in range(LANES):
                    v.wait_ge(maxed.sem[z], maxed.at(i, H1))
                    chain.link(v, i, v.tensor_copy(nparts[z][:, :, 0:H1], nmax[z][:, :, :]))
                    chain.link(v, i, v.tensor_tensor(nres[z][:, :, :], nmax[z][:, :, :], nparts[z][:, :, 0:H1],
                                                     ALU.subtract))
                    chain.link(v, i, v.tensor_copy(nparts[z][:, :, 1 * H1:2 * H1], nres[z][:, :, :]))
                    v.tensor_tensor(nparts[z][:, :, 2 * H1:3 * H1], nres[z][:, :, :], nparts[z][:, :, 1 * H1:2 * H1],
                                    ALU.subtract).then_inc(nm_parts.sem[z], 1)
                for g in range(4):
                    for z in range(LANES):
                        v.wait_ge(u_tr.sem[z], u_tr.at(i, g + 1))
                        heads = bank[z][3].rearrange("p (t c e) -> p t c e", t=NT, c=4)
                        chain.link(v, i, v.reciprocal(rec1[z][:, :, :], heads[:, :, :, E1]))
                        for half in range(2):
                            c = (2 * half + 2 * z) % 4
                            dst = MG[z][:, :, (4 * g + 2 * half) * E1:(4 * g + 2 * half + 2) * E1]
                            ins = v.tensor_tensor(dst.rearrange("p t (c e) -> p t c e", c=2),
                                                  heads[:, :, c:c + 2, 0:E1],
                                                  rec1[z][:, :, c:c + 2].unsqueeze(3).to_broadcast([P, NT, 2, E1]),
                                                  ALU.mult)
                        ins.then_inc(mg_ready.sem[z], 1)
                for z in range(LANES):
                    v.wait_ge(x_in[z].sem, x_in[z].now(i))
                    v.wait_ge(wo_done.sem[z], wo_done.at(i, 1))
                    v.tensor_tensor(X[z][:, :, :].rearrange("p t d -> p (t d)"), bank[z][1],
                                    X[z][:, :, :].rearrange("p t d -> p (t d)"), ALU.add).then_inc(x1_ready.sem[z], 1)
                for z in range(LANES):
                    v.wait_ge(x1_ready.sem[z], x1_ready.at(i, 1))
                moments(i, lambda z, tt: [X[z][:, tt, :]], this)
                for z in range(LANES):
                    normalise(i, z, Z, lambda z, tt: [X[z][:, tt, :]], this, 0)

                def rotate(l, tt, w):
                    for z in range(LANES):
                        if w == 0:
                            v.wait_ge(qk_done.sem[z], qk_done.at(i, tt + 1, l))
                            if tt:
                                v.wait_ge(k_ready.sem[z], k_ready.at(i, tt, l))
                        else:
                            v.wait_ge(k_squared.sem[z], k_squared.at(i, tt + 1, l))
                        src = bank[z][w].rearrange("p (h e) -> p h e", h=H2)
                        dc = RC[z][:, w, :].rearrange("p (h e) -> p h e", h=H2)
                        ds = RS[z][:, w, :].rearrange("p (h e) -> p h e", h=H2)
                        v.tensor_tensor(dc, src, rot[:, l, 2 * w, tt:tt + 1, :].to_broadcast([P, H2, E2]), ALU.mult)
                        for s in range(2):
                            o, n = 32 * s, 32 * (1 - s)
                            ins = v.tensor_tensor(
                                ds[:, :, o:o + 32], src[:, :, n:n + 32],
                                rot[:, l, 2 * w + 1, tt:tt + 1, o:o + 32].to_broadcast([P, H2, 32]), ALU.mult)
                        ins.then_inc((rot_done if w else q_rot).sem[z], 1)

                def norms(l, tt):
                    for z in range(LANES):
                        v.wait_ge(squared.sem[z], squared.at(i, tt + 1, l))
                        if tt:
                            v.wait_ge(inv_ready.sem[z], inv_ready.at(i, tt, l))
                        chain.link(v, i, v.tensor_reduce(
                            ss[z][:, :], SQ[z][:, :, :].rearrange("p w (h e) -> p (w h) e", e=E2), AX.X, ALU.add))
                        v.tensor_scalar(ss[z][:, :], ss[z][:, :], 1e-24, None, ALU.max).then_inc(ss_ready.sem[z], 1)

                def q_over(l, tt):
                    for z in range(LANES):
                        v.wait_ge(q_tr.sem[z], q_tr.at(i, tt + 1, l))
                        if tt:
                            v.wait_ge(s2_done.sem[z], s2_done.at(i, tt * PAIR2, l))
                        for s in range(2):
                            ins = v.tensor_copy(QT[z][s * E2:(s + 1) * E2, s, :, :],
                                                bank[z][1][s * E2:(s + 1) * E2, :].rearrange("p (j q) -> p j q", j=PAIR2))
                        ins.then_inc(qt_ready.sem[z], 1)

                def maxima(l, u):
                    tt, j, b = u // PAIR2, u % PAIR2, 2 * (u % 2)
                    for z in range(LANES):
                        v.wait_ge(s2_done.sem[z], s2_done.at(i, u + 1, l))
                        if j == 0:
                            v.wait_ge(inv_ready.sem[z], inv_ready.at(i, tt + 1, l))
                        chain.link(v, i, v.tensor_reduce(
                            nm2[z][:, b:b + 2], bank[z][2][:, 0:2 * KEYS].rearrange("p (h c) -> p h c", h=2),
                            AX.X, ALU.max, negate=True))
                        v.tensor_tensor(nb2[z][:, b:b + 2], nm2[z][:, b:b + 2], inv[z][:, tt % 2, 2 * j:2 * j + 2],
                                        ALU.mult).then_inc(nb2_ready.sem[z], 1)

                def probabilities(l, u):
                    b = 2 * (u % 2)
                    for z in range(LANES):
                        v.wait_ge(exp2.sem[z], exp2.at(i, u + 1, l))
                        chain.link(v, i, v.reciprocal(rec2[z][:, b:b + 2], sum2[z][:, b:b + 2]))
                        if u >= 2:
                            v.wait_ge(p_tr.sem[z], p_tr.at(i, u - 1, l))
                        if u >= PAIR2:
                            v.tensor_tensor(PP[z][:, u % 2, :].rearrange("p (h c) -> p h c", h=2),
                                            PR[z][:, u % 2, :, 0:WIN],
                                            rec2[z][:, b:b + 2].unsqueeze(2).to_broadcast([P, 2, WIN]), ALU.mult)
                        v.tensor_tensor(PM[z][:, u % 2, :].rearrange("p (h c) -> p h c", h=2),
                                        PR[z][:, u % 2, :, WIN:KEYS],
                                        rec2[z][:, b:b + 2].unsqueeze(2).to_broadcast([P, 2, P]),
                                        ALU.mult).then_inc(p_ready.sem[z], 1)

                def add_heads(l, tt):
                    for z in range(LANES):
                        v.wait_ge(wo2_done.sem[z], wo2_done.at(i, tt + 1, l))
                        v.tensor_tensor(Z[z][:, tt, :], bank[z][1][:, 0:D], Z[z][:, tt, :],
                                        ALU.add).then_inc(z_acc.sem[z], 1)

                for l in range(L):
                    for z in range(LANES):
                        v.memset(KT[z][:, :, 0:WIN], 0.0).then_inc(pad_ready.sem[z], 1)
                    rotate(l, 0, 0)
                    rotate(l, 0, 1)
                    norms(l, 0)
                    q_over(l, 0)
                    for tt in range(NT):
                        for k in range(PAIR2):
                            u = tt * PAIR2 + k
                            maxima(l, u)
                            if tt < NT - 1:
                                if k == 1:
                                    rotate(l, tt + 1, 1)
                                if k == 2:
                                    norms(l, tt + 1)
                            probabilities(l, u)
                            if tt < NT - 1 and k == 0:
                                rotate(l, tt + 1, 0)
                            if tt >= 1 and k == 2:
                                add_heads(l, tt - 1)
                            if tt < NT - 1 and k == 3:
                                q_over(l, tt + 1)
                            if l == L - 1:
                                if u == UNITS - PAIR2 - 1:
                                    next_moments(Next(i), i)
                                if u == UNITS - PAIR2:
                                    next_normalise(Next(i))
                                if u == UNITS - 3:
                                    next_rope(Next(i), 0)
                                if u == UNITS - 2:
                                    next_sum(Next(i), 0)
                                if u == UNITS - 1:
                                    next_rope(Next(i), 1)
                                    next_rest(Next(i), 0)
                    if l == L - 1:
                        next_low(Next(i), 0)
                    add_heads(l, NT - 1)
                    halves = lambda z, tt: [Z[z][:, tt, 0:64], bank[z][2][:, tt * 64:(tt + 1) * 64]]
                    if l == L - 1:
                        next_sum(Next(i), 1)
                    for z in range(LANES):
                        v.wait_ge(shifted.sem[z], shifted.at(i, 1, l))
                    moments(i, halves, this)
                    if l == L - 1:
                        next_rest(Next(i), 1)
                    for z in range(LANES):
                        if l == 0:
                            v.wait_ge(y_out[z].sem, 1 + y_out[z].before(i))
                        normalise(i, z, XN, halves, this, 1 + l)
                    if l == L - 1:
                        next_low(Next(i), 1)
                    for z in range(LANES):
                        for c, (c0, w) in enumerate(CH):
                            v.wait_ge(up_mm.sem[z], up_mm.at(i, c + 1, l))
                            v.wait_ge(gelu.sem[z], gelu.at(i, c + 1, l))
                            v.scalar_tensor_tensor(out=G[z][0:w, c, :], in0=bank[z][c][0:w, :],
                                                   scalar=b1[0:w, l, 0, c:c + 1], in1=G[z][0:w, c, :],
                                                   op0=ALU.add, op1=ALU.mult).then_inc(hid.sem[z], 1)
                    for z in range(LANES):
                        v.wait_ge(down_mm.sem[z], down_mm.at(i, 1, l))
                        v.wait_ge(z_b2.sem[z], z_b2.at(i, 1, l))
                        zf = Z[z][:, :, :].rearrange("p t d -> p (t d)")
                        v.tensor_tensor(zf, bank[z][3], zf, ALU.add).then_inc(z_out.sem[z], 1)
                for z in range(LANES):
                    v.wait_ge(z_out.sem[z], z_out.at(i, 1, L - 1))
                    v.tensor_tensor(XN[z][:, :, :], X[z][:, :, :], Z[z][:, :, :], ALU.add).then_inc(fin.sem[z], 1)
            assert chain.count - before_loop == DVE_ORDER, chain.count - before_loop

        @block.scalar
        def _(a):
            a.wait_ge(consts, 16 * (N_CONST + L * 8))
            a.wait_ge(made, N_MADE)
            def next_x_over(n):
                for z in range(LANES):
                    a.wait_ge(next_tr.sem[z], next_tr.at(n, 1))
                    a.copy(XT_next[z], bank[z][0]).then_inc(next_xt.sem[z], 1)

            def next_high(n, w):
                for z in range(LANES):
                    a.wait_ge(rope_sum.sem[z], rope_sum.at(n, w + 1))
                    a.copy(qkp[z][:, w, 0, :], rope_t[z][:, w, :]).then_inc(part_hi.sem[z], 1)

            def next_middle(n, w):
                for z in range(LANES):
                    a.wait_ge(part_res.sem[z], part_res.at(n, w + 1))
                    a.copy(qkp[z][:, w, 1, :], rope_s[z][:, w, :]).then_inc(part_mid.sem[z], 1)

            def next_v_over(n):
                for z in range(LANES):
                    a.wait_ge(v1_done.sem[z], v1_done.at(n, 1))
                    a.copy(V1[z][:, :, 0:H1 * VW].rearrange("p t (h e) -> p t h e", h=H1)[:, :, :, 0:E1],
                           bank[z][0].rearrange("p (t h e) -> p t h e", t=NT, h=H1)).then_inc(v1_ready.sem[z], 1)

            next_x_over(0)
            next_high(0, 0)
            next_high(0, 1)
            next_middle(0, 0)
            next_middle(0, 1)
            next_v_over(0)
            with a.Fori(0, PAIRS) as i:
                for z in range(LANES):
                    a.wait_ge(nm_tr.sem[z], nm_tr.at(i, 1))
                    a.copy(NMT[z], bank[z][3][:, 0:256].bitcast(BF16)).then_inc(nmt_ready.sem[z], 1)

                def evacuate(g):
                    for z in range(LANES):
                        a.wait_ge(pv_done.sem[z], pv_done.at(i, 2 * g + 2))
                        a.copy(U[z], bank[z][3]).then_inc(u_ready.sem[z], 1)

                for h in range(H1):
                    for z in range(LANES):
                        a.wait_ge(scored_t.sem[z], scored_t.at(i, h + 1))
                        if h >= 4:
                            a.wait_ge(pv_done.sem[z], pv_done.at(i, (h - 4) // 2 + 1))
                        a.activation(PT1[z][:, h % 4, :], region[z][:, 0:SCORES], ACT.Exp,
                                     scale=SCALE1).then_inc(exped.sem[z], 1)
                    if h % 4 == 0 and h >= 4:
                        evacuate(h // 4 - 1)
                evacuate(3)
                for z in range(LANES):
                    a.wait_ge(tr_done.sem[z], tr_done.at(i, 1, 0))
                    a.copy(XT[z], bank[z][0]).then_inc(xt_ready.sem[z], 1)

                def squares(l, tt):
                    for z in range(LANES):
                        a.wait_ge(qk_done.sem[z], qk_done.at(i, tt + 1, l))
                        if tt:
                            a.wait_ge(ss_ready.sem[z], ss_ready.at(i, tt, l))
                        a.activation(SQ[z][:, 1, :], bank[z][1], ACT.Square).then_inc(k_squared.sem[z], 1)
                        a.wait_ge(q_rot.sem[z], q_rot.at(i, tt + 1, l))
                        a.activation(SQ[z][:, 0, :], bank[z][0], ACT.Square).then_inc(squared.sem[z], 1)

                def v_over(l, tt):
                    for z in range(LANES):
                        a.wait_ge(v_done.sem[z], v_done.at(i, tt + 1, l))
                        if tt > 1:
                            a.wait_ge(pv2.sem[z], pv2.at(i, (tt - 1) * PAIR2, l))
                        a.copy(V2[z][:, tt % 2, :], bank[z][0])
                        last64 = bank[z][0][64:128, :].rearrange("p (j s e) -> p j s e", j=PAIR2, s=2)
                        a.copy(VPB[z][64:128, tt % 3, :, 64:128], last64[:, :, 1, :])
                        a.copy(VPB[z][0:64, tt % 3, :, 0:64], last64[:, :, 0, :]).then_inc(v2_ready.sem[z], 1)

                def k_over(l, tt):
                    for z in range(LANES):
                        a.wait_ge(k_tr.sem[z], k_tr.at(i, tt + 1, l))
                        a.copy(KT[z][:, :, WIN + tt * P:WIN + (tt + 1) * P],
                               bank[z][0].rearrange("p (j q) -> p j q", j=PAIR2)).then_inc(kt_ready.sem[z], 1)

                def exps(l, u):
                    tt, j, b = u // PAIR2, u % PAIR2, 2 * (u % 2)
                    for z in range(LANES):
                        a.wait_ge(nb2_ready.sem[z], nb2_ready.at(i, u + 1, l))
                        if u >= 2:
                            a.wait_ge(p_ready.sem[z], p_ready.at(i, u - 1, l))
                        for s in range(2):
                            ins = a.activation(PR[z][:, u % 2, s, :], bank[z][2][:, s * KEYS:(s + 1) * KEYS], ACT.Exp,
                                               bias=nb2[z][:, b + s:b + s + 1],
                                               scale=inv[z][:, tt % 2, 2 * j + s:2 * j + s + 1],
                                               accum_out=sum2[z][:, b + s:b + s + 1])
                        ins.then_inc(exp2.sem[z], 1)

                def p_over(l, u):
                    w = (3 if u >= PAIR2 else 2) * P
                    for z in range(LANES):
                        a.wait_ge(p_tr.sem[z], p_tr.at(i, u + 1, l))
                        if u:
                            a.wait_ge(pv2.sem[z], pv2.at(i, u, l))
                        a.copy(PT[z][:, u % 2, 0:w], bank[z][3][:, 0:w]).then_inc(pt_ready.sem[z], 1)

                def o_over(l, u):
                    for z in range(LANES):
                        a.wait_ge(pv2.sem[z], pv2.at(i, u + 1, l))
                        if u >= PAIR2:
                            a.wait_ge(wo2_done.sem[z], wo2_done.at(i, u // PAIR2, l))
                        a.copy(OT[z][:, u % PAIR2, :], bank[z][3][:, 3 * P:4 * P]).then_inc(ot_ready.sem[z], 1)

                for l in range(L):
                    for z in range(LANES):
                        a.wait_ge(zt_tr.sem[z], zt_tr.at(i, 1, l))
                        a.copy(ZT[z][0:64, :], bank[z][0][0:64, :])
                        a.copy(ZT[z][64:128, 1:S], bank[z][0][64:128, 0:S - 1]).then_inc(zt_ready.sem[z], 1)
                    squares(l, 0)
                    v_over(l, 0)
                    k_over(l, 0)
                    for tt in range(NT):
                        for k in range(PAIR2):
                            u = tt * PAIR2 + k
                            exps(l, u)
                            if u >= 1:
                                p_over(l, u - 1)
                            if u >= 2:
                                o_over(l, u - 2)
                            if tt < NT - 1:
                                if k == 0:
                                    squares(l, tt + 1)
                                if k == 2:
                                    v_over(l, tt + 1)
                                if k == 3:
                                    k_over(l, tt + 1)
                            elif l == L - 1:
                                if k == 0:
                                    next_x_over(Next(i))
                                if k == 2:
                                    next_high(Next(i), 0)
                                if k == 3:
                                    next_middle(Next(i), 0)
                    p_over(l, UNITS - 1)
                    o_over(l, UNITS - 2)
                    o_over(l, UNITS - 1)
                    if l == L - 1:
                        next_v_over(Next(i))
                        next_high(Next(i), 1)
                        next_middle(Next(i), 1)
                    for z in range(LANES):
                        a.wait_ge(tr_done.sem[z], tr_done.at(i, 1, 1 + l))
                        a.activation(XT[z], bank[z][0], ACT.Identity, scale=lgb[:, l, 0:1],
                                     bias=lgb[:, l, 1:2]).then_inc(xt_ready.sem[z], 1)
                    for z in range(LANES):
                        for c, (c0, w) in enumerate(CH):
                            a.wait_ge(gate_mm.sem[z], gate_mm.at(i, c + 1, l))
                            a.activation(G[z][0:w, c, :], bank[z][1 + c][0:w, :], ACT.Gelu,
                                         bias=b1[0:w, l, 1, c:c + 1]).then_inc(gelu.sem[z], 1)

        @block.gpsimd
        def _(g):
            for z in range(LANES):
                g.memset(XN[z][:, 0, 0:1], 0.0).then_inc(y_out[z].sem, 1)
                g.memset(V1[z][:, :, :], 1.0).then_inc(made, 1)
                g.memset(ZT[z][:, 0:1], 0.0).then_inc(made, 1)
                g.memset(nparts[z][:, :, :], 0.0).then_inc(made, 1)
                g.memset(QT[z][:, :, :, :], 0.0).then_inc(made, 1)
                g.memset(VPB[z][:, :, :, :], 0.0).then_inc(made, 1)
            g.memset(nhalf[:, :], -0.5).then_inc(made, 1)
            g.wait_ge(made, N_MADE)

            def next_root(n):
                for z in range(LANES):
                    g.wait_ge(next_var.sem[z], next_var.at(n, 1))
                    g.tensor_tensor(rstd_next[z][:, :], veps_next[z][:, :], nhalf[:, 0:NT],
                                    ALU.pow).then_inc(next_rstd.sem[z], 1)

            next_root(0)
            with g.Fori(0, PAIRS) as i:
                def root(z, use):
                    g.wait_ge(ln_var.sem[z], ln_var.at(i, 1, use))
                    g.tensor_tensor(rstd[z][:, :], veps[z][:, :], nhalf[:, 0:NT], ALU.pow).then_inc(ln_rstd.sem[z], 1)

                for z in range(LANES):
                    root(z, 0)
                for l in range(L):
                    for tt in range(NT):
                        for z in range(LANES):
                            g.wait_ge(q_rot.sem[z], q_rot.at(i, tt + 1, l))
                            if tt:
                                g.wait_ge(q_tr.sem[z], q_tr.at(i, tt, l))
                            g.tensor_tensor(QR[z][:, 0, :], RC[z][:, 0, :], RS[z][:, 0, :], ALU.add).then_inc(q_ready.sem[z], 1)
                        for z in range(LANES):
                            g.wait_ge(rot_done.sem[z], rot_done.at(i, tt + 1, l))
                            g.tensor_tensor(RC[z][:, 1, :], RC[z][:, 1, :], RS[z][:, 1, :], ALU.add)
                        for z in range(LANES):
                            g.wait_ge(ss_ready.sem[z], ss_ready.at(i, tt + 1, l))
                            if tt > 1:
                                g.wait_ge(exp2.sem[z], exp2.at(i, (tt - 1) * PAIR2, l))
                            g.tensor_tensor(inv[z][:, tt % 2, :], ss[z][:, :], nhalf[:, :], ALU.pow).then_inc(inv_ready.sem[z], 1)
                            g.wait_ge(inv_ready.sem[z], inv_ready.at(i, tt + 1, l))
                            if tt:
                                g.wait_ge(k_tr.sem[z], k_tr.at(i, tt, l))
                            g.tensor_tensor(QR[z][:, 1, :].rearrange("p (h e) -> p h e", h=H2),
                                            RC[z][:, 1, :].rearrange("p (h e) -> p h e", h=H2),
                                            inv[z][:, tt % 2, H2:2 * H2].unsqueeze(2).to_broadcast([P, H2, E2]),
                                            ALU.mult).then_inc(k_ready.sem[z], 1)
                    if l == L - 1:
                        next_root(Next(i))
                    for z in range(LANES):
                        root(z, 1 + l)
                    for z in range(LANES):
                        g.wait_ge(ln_out.sem[z], ln_out.at(i, 1, 1 + l))
                        g.tensor_tensor(Z[z][:, :, :], Z[z][:, :, :], b2[:, l:l + 1, :].to_broadcast([P, NT, D]),
                                        ALU.add).then_inc(z_b2.sem[z], 1)


def constants():
    f = np.float32
    bf = mybir.dt.np(BF16)
    q, k = np.arange(P)[:, None], np.arange(P)[None, :]
    c = np.arange(KEYS)[None, :]
    seen = (c >= q) & (c <= q + WIN)
    const = {
        "ident": np.eye(P, dtype=f), "identb": np.eye(P, dtype=bf),
        "causal": np.where(k > q, f(NEG), f(0)).astype(bf), "causal_t": np.where(q > k, f(NEG), f(0)).astype(bf),
        "band": np.where(seen, f(0), f(NEG)).astype(bf), "band0": np.where(seen & (c >= WIN), f(0), f(NEG)).astype(bf),
        "shift": np.eye(P, k=1, dtype=f), "corner": ((q == P - 1) & (k == 0)).astype(f),
        "ones": np.ones((SPLIT, H1 * S), bf),
    }
    freqs = (f(1.0) / f(10000.0) ** (np.arange(0, E1, 2, dtype=f) / f(E1))).astype(f)
    angle = np.arange(S, dtype=f)[:, None] * freqs[None, :]
    e = np.arange(P) // H1
    const["cos1"] = np.cos(angle).astype(f)[:, e // 2].T
    const["sin1"] = (np.sin(angle).astype(f)[:, e // 2] * np.where(e % 2, f(1), f(-1))).T
    half = np.arange(0, E2, 2, dtype=f)
    tok = np.arange(S, dtype=f)
    angle = tok[:, None] * (f(1.0) / f(10000.0) ** (half / f(E2)))[None, :]
    angle = np.concatenate([angle, angle], -1)
    base = (half + f(0.4 * E2)) / f(1.4 * E2)
    scale = base[None, :] ** ((tok - S // 2) / f(WIN // 2))[:, None]
    scale = np.concatenate([scale, scale], -1)
    sign = np.where(np.arange(E2) < E2 // 2, f(-1), f(1))
    cos, sin = np.cos(angle), np.sin(angle) * sign
    rot = np.stack([cos * scale * f(8), sin * scale * f(8), cos / scale, sin / scale])
    const["rot"] = rot.reshape(4, NT, P, E2).transpose(2, 0, 1, 3)
    return {n: np.ascontiguousarray(v, v.dtype if v.dtype == bf else f) for n, v in const.items()}


def kernel(**inputs):
    import concourse.bacc as bacc
    from concourse.bass_utils import run_bass_kernel_spmd as run

    a = {n.replace("L0_attn_", "a_").replace("L0_ffn_", "f_"): np.asarray(v) for n, v in inputs.items()}
    turned = np.arange(E1) ^ 1

    def by_width(w, order):
        return w.reshape(H1, E1, D)[:, order].transpose(2, 1, 0).reshape(D, D)

    same = np.arange(E1)
    swapped = np.roll(np.arange(E2), E2 // 2)
    b1 = np.zeros((P, L, 2, 3), a["f_b1"].dtype)
    for c, (c0, w) in enumerate(CH):
        for s in range(2):
            b1[0:w, :, s, c] = a["f_b1"][:, s * HID + c0:s * HID + c0 + w].T
    arrays = {
        "x": np.concatenate([a["a_x"], a["a_x"][:LANES]]),
        "w1st": np.stack([by_width(a["a_wq"], same), by_width(a["a_wq"], turned), by_width(a["a_wk"], same),
                          by_width(a["a_wk"], turned), a["a_wv"].T, a["a_wo"].T], axis=1),
        "wqkv": a["f_wqkv"], "wo2": a["f_wo"], "w1": a["f_w1"], "w2": a["f_w2"], "b1": b1, "b2": a["f_b2"],
        "lgb": np.stack([a["f_ln_g"].T, a["f_ln_b"].T], axis=2),
        "scl": np.stack([a["f_q_scale"], a["f_q_scale"][:, swapped], a["f_k_scale"], a["f_k_scale"][:, swapped]], axis=1),
    }
    arrays.update(constants())
    arrays = {f"in_{n}": np.ascontiguousarray(v) for n, v in arrays.items()}
    nc = bacc.Bacc("TRN2", target_bir_lowering=False, num_devices=1)
    t = {n[3:]: nc.dram_tensor(n, v.shape, mybir.dt.from_np(v.dtype), kind="ExternalInput").ap()
         for n, v in arrays.items()}
    out = nc.dram_tensor("out", (B, S, D), F32, kind="ExternalOutput").ap()
    build(nc, t, out)
    return run(nc, [arrays], core_ids=[0]).results[0]["out"]
```
